# Optimizing a Trainium2 kernel written in Bass

```python
import numpy as np
import jax
import jax.numpy as jnp

def _softmax(x, axis=-1):
    return jax.nn.softmax(x, axis=axis)

def _gelu(x):
    return jax.nn.gelu(x, approximate=True)

def _silu(x):
    return jax.nn.silu(x)

def _sigmoid(x):
    return jax.nn.sigmoid(x)

def _layernorm(x, axis=-1, eps=1e-05):
    m = jnp.mean(x, axis=axis, keepdims=True)
    v = jnp.var(x, axis=axis, keepdims=True)
    return (x - m) / jnp.sqrt(v + eps)

def _scatter_add(tgt, idx, src, axis=0):
    return tgt.at[idx].add(src)

def _segment_sum(src, seg, n):
    return jax.ops.segment_sum(src, seg, n)
kernel_name = 'mk_flamingo_gated_d1_seqx_r4_3d1105'

def setup_inputs(seed: int=0):
    np.random.seed(seed)
    _w = jnp.asarray

    def _rec_inputs():
        import jax
        import jax.numpy as jnp
        _rk = jax.random.key(seed)
        x = -0.000125 + 0.9999 * jax.random.normal(jax.random.fold_in(_rk, 1), (2, 512, 1024), jnp.float32)
        _lenS = 512 - jax.random.randint(jax.random.fold_in(_rk, 7), (2,), 0, max(1, 512 // 4) + 1, jnp.int32)
        _lenS2 = 1024 - jax.random.randint(jax.random.fold_in(_rk, 8), (2,), 0, max(1, 1024 // 4) + 1, jnp.int32)
        _ctx_4096P = jax.random.normal(jax.random.fold_in(_rk, 11), (2, 16, 1024), jnp.float32)
        _ctx_4096c = jax.random.dirichlet(jax.random.fold_in(_rk, 511), 0.3 * jnp.ones((16,), jnp.float32), (2, 1024))
        _ctx_4096t = jnp.einsum('bsk,bkd->bsd', _ctx_4096c, _ctx_4096P)
        _ctx_4096t = _ctx_4096t * jax.lax.rsqrt(jnp.mean(jnp.square(_ctx_4096t)) + 1e-12) * 0.953939
        ctx_4096 = -5.72187e-05 + 0.999849 * (_ctx_4096t + 0.3 * jax.random.normal(jax.random.fold_in(_rk, 611), (2, 1024, 1024), jnp.float32))
        _g = jax.random.normal(jax.random.fold_in(_rk, 9001), (2, 1), jnp.float32)
        _g = jnp.sign(_g) * jnp.maximum(jnp.abs(_g), 1.0) + (_g == 0) * 1.0
        g_xattn = _g[0]
        g_ffn = _g[1]
        return (x, ctx_4096, g_xattn, g_ffn)
    x, ctx_4096, g_xattn, g_ffn = _rec_inputs()

    def _L0_xattn_setup():
        import jax, jax.numpy as jnp
        import numpy as np
        QMIN = 0.0
        QMAX = 255.0

        def fake_quant(x, scale, zp):
            s = scale.reshape(())
            z = zp.reshape(())
            q = jnp.clip(jnp.round(x / s + z), QMIN, QMAX)
            return (q - z) * s
        key = jax.random.key(seed)
        k1, k2 = jax.random.split(key)
        B, M, K, N = (4, 512, 1024, 1024)
        x1 = jax.random.normal(k1, (B, M, K), dtype=jnp.float32)
        x2 = jax.random.normal(k2, (B, K, N), dtype=jnp.float32)
        x1_scale = jnp.full((1,), 8.0 / 255.0, dtype=jnp.float32)
        x1_zp = jnp.full((1,), 128.0, dtype=jnp.float32)
        x2_scale = jnp.full((1,), 8.0 / 255.0, dtype=jnp.float32)
        x2_zp = jnp.full((1,), 128.0, dtype=jnp.float32)
        return {'x1': x1, 'x2': x2, 'x1_scale': x1_scale, 'x1_zp': x1_zp, 'x2_scale': x2_scale, 'x2_zp': x2_zp}
    _L0_xattn_all = _L0_xattn_setup()
    _L0_xattn_in = {k: v for k, v in _L0_xattn_all.items() if k in ('x1_scale', 'x1_zp', 'x2_scale', 'x2_zp')}
    del _L0_xattn_all

    def _L0_ffn_setup():
        import jax, jax.numpy as jnp
        import numpy as np
        TOP_K = 2
        key = jax.random.key(seed)
        k0, k1, k2 = jax.random.split(key, 3)
        B, S, D, H, E = (4, 512, 1024, 1024, 8)
        sc = 1.0 / np.sqrt(D).astype(np.float32)
        x = jax.random.normal(k0, (B, S, D), dtype=jnp.float32)
        W_gate = jax.random.normal(k1, (D, E), dtype=jnp.float32) * sc
        b_gate = jnp.zeros((E,), dtype=jnp.float32)
        W_e = jax.random.normal(k2, (E, D, H), dtype=jnp.float32) * sc
        b_e = jnp.zeros((E, H), dtype=jnp.float32)
        return {'x': x, 'W_gate': W_gate, 'b_gate': b_gate, 'W_e': W_e, 'b_e': b_e}
    _L0_ffn_all = _L0_ffn_setup()
    _L0_ffn_in = {k: v for k, v in _L0_ffn_all.items() if k in ('W_gate', 'b_gate', 'W_e', 'b_e')}
    del _L0_ffn_all
    return {'x': x, 'ctx_4096': ctx_4096, 'g_xattn': g_xattn, 'g_ffn': g_ffn, 'L0_xattn_x1_scale': _L0_xattn_in['x1_scale'], 'L0_xattn_x1_zp': _L0_xattn_in['x1_zp'], 'L0_xattn_x2_scale': _L0_xattn_in['x2_scale'], 'L0_xattn_x2_zp': _L0_xattn_in['x2_zp'], 'L0_ffn_W_gate': _L0_ffn_in['W_gate'], 'L0_ffn_b_gate': _L0_ffn_in['b_gate'], 'L0_ffn_W_e': _L0_ffn_in['W_e'], 'L0_ffn_b_e': _L0_ffn_in['b_e']}

def reference(x, ctx_4096, g_xattn, g_ffn, L0_xattn_x1_scale, L0_xattn_x1_zp, L0_xattn_x2_scale, L0_xattn_x2_zp, L0_ffn_W_gate, L0_ffn_b_gate, L0_ffn_W_e, L0_ffn_b_e):
    import jax
    import jax.numpy as jnp

    def _L0_xattn_ref(x1, x2, x1_scale, x1_zp, x2_scale, x2_zp):
        import jax, jax.numpy as jnp
        import numpy as np
        QMIN = 0.0
        QMAX = 255.0

        def fake_quant(x, scale, zp):
            s = scale.reshape(())
            z = zp.reshape(())
            q = jnp.clip(jnp.round(x / s + z), QMIN, QMAX)
            return (q - z) * s
        q1 = fake_quant(x1, x1_scale, x1_zp)
        q2 = fake_quant(x2, x2_scale, x2_zp)
        return jnp.matmul(q1, q2)

    def _L0_ffn_ref(x, W_gate, b_gate, W_e, b_e):
        import jax, jax.numpy as jnp
        import numpy as np
        TOP_K = 2
        logits = x @ W_gate + b_gate
        _, top_idx = jax.lax.top_k(logits, TOP_K)
        y_all = jax.nn.relu(jnp.einsum('bsd,edh->bseh', x, W_e) + b_e)
        y = jnp.take_along_axis(y_all, top_idx[..., None], axis=2)
        return y.mean(axis=2)
    x = x + jnp.tanh(g_xattn[0]) * _L0_xattn_ref(_layernorm(x, axis=-1), ctx_4096, L0_xattn_x1_scale, L0_xattn_x1_zp, L0_xattn_x2_scale, L0_xattn_x2_zp)
    x = x + jnp.tanh(g_ffn[0]) * _L0_ffn_ref(_layernorm(x, axis=-1), L0_ffn_W_gate, L0_ffn_b_gate, L0_ffn_W_e, L0_ffn_b_e)
    return x

_drawn_inputs = setup_inputs


def setup_inputs(seed=0):
    import zlib

    import numpy as np

    out = dict(_drawn_inputs(seed))
    spreads = {'L0_ffn_b_gate': (0.0, 2.0), 'L0_ffn_b_e': (0.0, 2.0)}
    factors = {'L0_ffn_W_gate': 3.593, 'L0_ffn_W_e': 3.073}
    for name, (base, spread) in spreads.items():
        noise = np.random.default_rng([zlib.crc32(name.encode()), seed]).standard_normal(out[name].shape)
        drawn = base * np.exp(spread * noise) if base else spread * noise
        out[name] = jnp.asarray(drawn.astype(out[name].dtype))
    for name, factor in factors.items():
        out[name] = (out[name] * factor).astype(out[name].dtype)
    return out
```

```python
import concourse.bass as bass
from concourse import mybir
from contextlib import ExitStack


def flamingo_gated_moe(nc, x, ctx_kv, g_xattn, g_ffn, x1_scale, x1_zp, x2_scale, x2_zp,
                       W_gate, b_gate, W_e, b_e, out):
    f32, f32r, bf16, f16 = mybir.dt.float32, mybir.dt.float32r, mybir.dt.bfloat16, mybir.dt.float16
    i32, u32, u8 = mybir.dt.int32, mybir.dt.uint32, mybir.dt.uint8
    ALU, ACT = mybir.AluOpType, mybir.ActivationFunctionType
    AX = mybir.AxisListType

    P = 128
    B, S, D = x.shape
    E = W_e.shape[0]
    KT = D // P
    NT = B * S // P
    TPB = S // P
    HB = D // 512
    TOPK = 2
    MAX_SLOTS = (TOPK * NT * P - E) // P + E
    NS = MAX_SLOTS + 3
    QMID = 128.0
    EPS = 1e-5
    WSZ = KT * D
    NCH = 4
    CK = KT // NCH
    CW = WSZ // NCH

    x_t = x.rearrange("b (n p) d -> (b n) p d", p=P)
    out_rows = out.rearrange("b s d -> (b s) d")
    out_t = out.rearrange("b (n p) d -> (b n) p d", p=P)
    ctx_t = ctx_kv.rearrange("b (k p) d -> (b k) p d", p=P)
    w_t = W_e.rearrange("e (k p) h -> p e k h", p=P)
    y_dram = nc.dram_tensor("y_scratch", (NT * P, D), f32, kind="Internal").ap()
    y_t = y_dram.rearrange("(n p) d -> n p d", p=P)

    ctx = ExitStack()
    with ctx:
        def sb(name, shape, dt):
            return ctx.enter_context(nc.sbuf_tensor(name, shape, dt))

        def sem(name):
            return ctx.enter_context(nc.semaphore(name))

        KB = 1024
        arena = sb("arena", [P, 200 * KB], u8)
        base = nc.sbuf_base - 200 * KB

        def at(name, shape, dt, off):
            return nc.alloc_sbuf_tensor_at(name, shape, dt, offset=base + off)

        WHI, WLO, STG, YT, GB, RES, BIA = 0, 64 * KB, 128 * KB, 160 * KB, 176 * KB, 184 * KB, 192 * KB
        w_hi = at("w_hi", [P, 2 * WSZ], f32r, WHI)
        w_lo = at("w_lo", [P, 2 * WSZ], f32r, WLO)
        stage = at("stage", [P, KT, D], f32, STG)
        yT_hi = [at(f"yT_hi{q}", [P, KT, P], f32r, YT + 4 * KB * q) for q in range(2)]
        yT_lo = [at(f"yT_lo{q}", [P, KT, P], f32r, YT + 8 * KB + 4 * KB * q) for q in range(2)]
        y_rows = [at(f"y_rows{q}", [P, D], f32, GB + 4 * KB * q) for q in range(2)]
        res = [at(f"res{q}", [P, D], f32, RES + 4 * KB * q) for q in range(2)]
        bias = at("bias", [P, 2 * D], f32, BIA)
        xt = at("xt", [P, NT, D], f32, WHI + 32 * KB)
        onehot = [at(f"onehot{i}", [P, E, P], bf16, WHI + 32 * KB + 4 * KB * i) for i in range(NT)]
        q1T = at("q1T", [P, NT, KT, P], bf16, WHI + 16 * KB)
        q2 = at("q2", [P, B * KT, D], bf16, WLO + 32 * KB)
        q1 = at("q1", [P, 2, D], bf16, RES)
        yT = [at(f"yT{q}", [P, KT, P], f32, YT + 4 * KB * q) for q in range(2)]
        y = [at(f"y{q}", [P, D], f32, GB + 4 * KB * q) for q in range(2)]
        CB = 6
        corr = stage[:, CB:CB + B, :]
        u8x = sb("u8x", [P, 2, D], u8)
        u8c = at("u8c", [P, 2, D], u8, RES + 4 * KB)

        ident_b = sb("ident_b", [P, P], bf16)
        ident_f = sb("ident_f", [P, P], f32)
        ones_b = at("ones_b", [P, P], bf16, YT + 8 * KB)
        before = at("before", [P, P], bf16, YT + 8 * KB + 256)
        iota_f = at("iota_f", [P, P], f32, YT + 8 * KB + 512)
        iota_b = at("iota_b", [P, P], bf16, YT + 9 * KB)
        wg = at("wg", [P, KT, E], f32, YT + 10 * KB)
        tri = at("tri", [P, E + 1, E], f32, YT + 10 * KB + 256)
        R = at("R", [P, NT, E, NS], f16, YT + 11 * KB)
        cmp = at("cmp", [P, NT, E, NS], f16, RES + 0)
        tok1 = sb("tok1", [P, NT], f32)
        tok1m2 = sb("tok1m2", [P, NT], f32)
        back = sb("back", [P, NT], f32)
        backm = sb("backm", [P, NT], f32)
        par = sb("par", [P, 6], f32)
        bg = sb("bg", [P, E], f32)
        drv = sb("drv", [P, 16], f32)
        INV1, INV2, D1, D2, C1, C1D1, C1D2, C1KDD, C2, TX, TF, TMP = range(12)

        def dv(c):
            return drv[:, c:c + 1]

        eps = sb("eps", [P, 1], f32)
        st = sb("st", [P, 2, 2, 6], f32)
        mv = sb("mv", [P, 2, NT, 2], f32)
        lnv = sb("lnv", [P, 2, NT, 8], f32)
        VE, STD, RST, T1, T2, NA, BB, AA = range(8)
        rsum = sb("rsum", [P, NT], f32)
        lg = sb("lg", [P, E], f32)
        pw = at("pw", [P, 4, E, E], f32, RES + 6 * KB)
        rank = sb("rank", [P, E], f32)
        sel = sb("sel", [P, NT, E], bf16)
        run = sb("run", [P, NT + 1, E], bf16)
        sgn = sb("sgn", [P, NT, E], f32)
        pos = sb("pos", [P, E], f32)
        pH = sb("pH", [P, NT, E], f32)
        pHi = sb("pHi", [P, E], u8)
        pL = sb("pL", [P, NT, E], bf16)
        cnt = sb("cnt", [P, 6, 9], f32)
        cnt8 = sb("cnt8", [P, E], u8)
        tri9 = sb("tri9", [P, E + 1, E], f32)
        sid = sb("sid", [P, NT, E], f32)
        sc26 = at("sc26", [P, NS, E], f32, RES + 7 * KB)
        sv = at("sv", [P, 6, NS], f32, RES + 5 * KB)
        svi = sb("svi", [P, NS], u8)
        tab = sb("tab", [P, 3 * NS + E + 1], i32)
        NEED, WOFF, NXT, BAS = 0, NS, 2 * NS, 3 * NS
        idx = sb("idx", [P, NS], u32)
        weight = sb("weight", [P, NS], f32)
        gidx = sb("gidx", [P, 2], u32)
        sidx = sb("sidx", [P, 2], u32)

        ps = [ctx.enter_context(nc.psum_tensor(f"ps{i}", [P, HB * 512], f32)) for i in range(2)]
        ps_q = ctx.enter_context(nc.psum_tensor("ps_q", [P, KT, P], bf16))
        ps_y = ctx.enter_context(nc.psum_tensor("ps_y", [P, KT, P], f32))
        ps_s = ctx.enter_context(nc.psum_tensor("ps_s", [P, 512], f32))
        RS_C, GT_C, CU_C, TO_C = 0, 8, 16, 24

        s_par = sem("params_landed")
        s_wg = sem("gate_landed")
        s_x = [sem(f"x_landed{i}") for i in range(NT)]
        s_ctx = [sem(f"ctx_landed{i}") for i in range(CB)]
        s_w = [sem(f"w_landed{c}") for c in range(NCH)]
        s_bias = [sem(f"bias_landed{q}") for q in range(2)]
        s_const = sem("consts_made")
        s_cstep = sem("const_step")
        s_tanh = sem("tanh_done")
        s_drv = sem("params_derived")
        s_v = sem("dve_step")
        s_var = [sem("var1_ready"), sem("var2_ready")]
        s_std = [sem("std1_ready"), sem("std2_ready")]
        s_ab = [sem("scale1_ready"), sem("scale2_ready")]
        s_u = sem("x_quantised")
        s_q1 = sem("q1_ready")
        s_qt = sem("q1T_in_psum")
        s_qe = sem("q1T_ready")
        s_uc = sem("ctx_quantised")
        s_q2 = sem("q2_ready")
        s_att = sem("attn_in_psum")
        s_small = sem("small_in_psum")
        s_sread = sem("small_read")
        s_corr = sem("corr_ready")
        s_xr = sem("x_plus_rowsum")
        s_xc = sem("x_plus_corr")
        s_xn = sem("x_new_ready")
        s_y = sem("y_ready")
        s_oi = sem("x_new_stored")
        s_ys = sem("y_stored")
        s_yt = sem("yT_in_psum")
        s_ye = sem("yT_ready")
        s_sel = sem("selection_ready")
        s_oh = sem("onehots_ready")
        s_R = sem("slot_matrix_ready")
        s_idx_ps = sem("indices_in_psum")
        s_idx = sem("indices_ready")
        s_tab = sem("schedule_ready")
        s_hi = sem("w_hi_done")
        s_lo = sem("w_lo_done")
        s_pool = sem("pool_step")
        s_g = [sem(f"gathered{q}") for q in range(2)]
        s_tp = sem("slot_yT_in_psum")
        s_eh = sem("slot_yT_hi_ready")
        s_el = sem("slot_yT_lo_ready")
        s_mm = sem("slot_matmuls_done")
        s_free = sem("slot_psum_free")
        s_post = sem("slot_result_ready")
        s_resf = sem("slot_result_free")
        s_sc = sem("slot_scattered")
        s_settled = sem("waits_settled")

        block = ctx.enter_context(nc.Block())

        def slots(eng, body):
            n_used = eng.value_load(tab[0:1, BAS + E:BAS + E + 1], min_val=E, max_val=MAX_SLOTS)
            with eng.Fori(0, (MAX_SLOTS + 1) // 2) as turn:
                for q in range(2):
                    with eng.If(turn * 2 + q < n_used):
                        body(turn * 2 + q, q, turn)
            return n_used

        def entry(eng, field, slot, hi):
            return eng.value_load(tab[0:1, bass.ds(slot + field, 1)], min_val=0, max_val=hi)

        def settle(eng):
            eng.sem_inc(s_settled, 1)

        @block.sync
        def _(sp):
            for c, src in enumerate((x1_scale, x1_zp, x2_scale, x2_zp, g_xattn, g_ffn)):
                sp.dma_start(par[:, c:c + 1], src.partition_broadcast(P)).then_inc(s_par, 16)
            sp.dma_start(bg[:, :], b_gate.partition_broadcast(P)).then_inc(s_par, 16)

            def load_ctx(k):
                if k >= CB:
                    sp.wait_ge(s_uc, k - CB + 1)
                sp.dma_start(stage[:, k % CB, :], ctx_t[k]).then_inc(s_ctx[k % CB], 16)

            def load_x(i):
                sp.dma_start(xt[:, i, :], x_t[i]).then_inc(s_x[i], 16)

            for i in range(TPB):
                load_x(i)
                load_ctx(i)
            for k in range(TPB, KT):
                load_ctx(k)
            sp.dma_start(wg[:, :, :], W_gate.rearrange("(k p) e -> p k e", p=P)).then_inc(s_wg, 16)
            for i in range(TPB):
                load_x(TPB + i)
                load_ctx(KT + i)
            for k in range(KT + TPB, 2 * KT):
                load_ctx(k)
            sp.wait_ge(s_uc, B * KT)
            for c in range(NCH):
                if c == NCH - 1:
                    sp.wait_ge(s_xc, NT)
                sp.dma_start(stage[:, CK * c:CK * (c + 1), :], w_t[:, 0, CK * c:CK * (c + 1), :]).then_inc(s_w[c], 16)
            for e in range(2):
                sp.dma_start(bias[:, e * D:(e + 1) * D], b_e[e].partition_broadcast(P)).then_inc(s_bias[e], 16)
            sp.wait_ge(s_tab, 1)
            with sp.Fori(1, E) as n:
                for c in range(NCH):
                    sp.wait_ge(s_hi, n * NCH - NCH + c + 1)
                    sp.wait_ge(s_lo, n * NCH - NCH + c + 1)
                    sp.dma_start(stage[:, CK * c:CK * (c + 1), :],
                                 w_t[:, bass.ds(n, 1), CK * c:CK * (c + 1), :].rearrange("p e k h -> p (e k) h")
                                 ).then_inc(s_w[c], 16)
                with sp.If(n > 1):
                    sp.wait_ge(s_post, entry(sp, BAS - 1, n, MAX_SLOTS))
                    settle(sp)
                    for q in range(2):
                        with sp.If((n & 1) == q):
                            sp.dma_start(bias[:, q * D:(q + 1) * D],
                                         b_e[bass.ds(n, 1), :].rearrange("a d -> (a d)").partition_broadcast(P)
                                         ).then_inc(s_bias[q], 16)
                    sp.nop()
                sp.nop()

        @block.gpsimd
        def _(pool):
            pool.memset(ident_b[:, :], 0.0)
            pool.memset(ident_f[:, :], 0.0)
            pool.memset(ones_b[:, :], 1.0)
            pool.memset(before[:, :], 1.0)
            pool.memset(tri[:, :, :], 1.0)
            pool.memset(eps[:, :], EPS)
            pool.memset(run[:, 0, :], 0.0)
            pool.iota(iota_f[:, :], [[1, P]], base=0, channel_multiplier=0, allow_small_or_imprecise_dtypes=True)
            pool.iota(iota_b[:, :], [[1, P]], base=0, channel_multiplier=0, allow_small_or_imprecise_dtypes=True)
            pool.iota(tok1[:, :], [[P, NT]], base=1, channel_multiplier=1, allow_small_or_imprecise_dtypes=True)
            pool.iota(tok1m2[:, :], [[-2 * P, NT]], base=-2, channel_multiplier=-2, allow_small_or_imprecise_dtypes=True)
            pool.iota(back[:, :], [[-P, NT]], base=NT * P - 1, channel_multiplier=-1, allow_small_or_imprecise_dtypes=True)
            pool.iota(backm[:, :], [[P, NT]], base=1 - NT * P, channel_multiplier=1,
                      allow_small_or_imprecise_dtypes=True).then_inc(s_cstep, 1)
            pool.wait_ge(s_cstep, 1)
            pool.affine_select(out=ident_b[:, :], in_=ident_b[:, :], compare_op=ALU.not_equal, fill=1.0,
                               base=0, pattern=[[-1, P]], channel_multiplier=1)
            pool.affine_select(out=ident_f[:, :], in_=ident_f[:, :], compare_op=ALU.not_equal, fill=1.0,
                               base=0, pattern=[[-1, P]], channel_multiplier=1)
            pool.affine_select(out=before[:, :], in_=before[:, :], compare_op=ALU.is_gt, fill=0.0,
                               base=0, pattern=[[1, P]], channel_multiplier=-1)
            pool.affine_select(out=tri[:, :, :], in_=tri[:, :, :], compare_op=ALU.is_gt, fill=0.0,
                               base=0, pattern=[[1, E + 1], [-1, E]], channel_multiplier=0).then_inc(s_const, 1)
            pool.sem_inc(s_resf, 2)

            def centre_ctx(k):
                pool.wait_ge(s_uc, k + 1)
                pool.tensor_scalar(q2[:, k, :], u8c[:, k % 2, :], 1.0, -QMID, ALU.mult, ALU.add).then_inc(s_q2, 1)

            def add_corr(i):
                pool.wait_ge(s_corr, i // TPB + 1)
                pool.wait_ge(s_xr, i + 1)
                pool.tensor_tensor(xt[:, i, :], xt[:, i, :], corr[:, i // TPB, :], ALU.add).then_inc(s_xc, 1)

            def split_lo(c):
                pool.wait_ge(s_hi, c + 1)
                pool.tensor_tensor(w_lo[:, c * CW:(c + 1) * CW], stage[:, CK * c:CK * (c + 1), :].rearrange("p k h -> p (k h)"),
                                   w_hi[:, c * CW:(c + 1) * CW].bitcast(f32), ALU.subtract).then_inc(s_lo, 1)

            for k in range(KT):
                centre_ctx(k)
            add_corr(0)
            for i in range(NT + 3):
                if i < TPB:
                    centre_ctx(KT + 2 * i)
                    centre_ctx(KT + 2 * i + 1)
                if i + 1 < NT:
                    add_corr(i + 1)
                if i == NT:
                    split_lo(0)
                if i == NT + 1:
                    split_lo(1)
            split_lo(2)
            split_lo(3)

            def gather(slot, q, step):
                pool.tensor_copy(gidx[:, q:q + 1], idx[:, bass.ds(slot, 1)]).then_inc(s_pool, 1)
                pool.wait_ge(s_pool, step)
                settle(pool)
                pool.indirect_dma_start(out=y_rows[q][:, :], out_offset=None, in_=y_dram[:, :],
                                        in_offset=bass.IndirectOffsetOnAxis(ap=gidx[:, q:q + 1], axis=0)
                                        ).then_inc(s_g[q], 16)

            pool.wait_ge(s_idx, 1)
            pool.wait_ge(s_tab, 1)
            pool.wait_ge(s_ys, 16 * NT)
            pool.wait_ge(s_oi, 16 * NT)
            for q in range(2):
                gather(q, q, q + 1)

            def step(slot, q, turn):
                pool.wait_ge(s_tp, slot + 1)
                gather(slot + 2, q, slot * 2 + 3)
                pool.tensor_copy(sidx[:, q:q + 1], idx[:, bass.ds(slot, 1)]).then_inc(s_pool, 1)
                pool.wait_ge(s_pool, slot * 2 + 4)
                pool.wait_ge(s_post, slot + 1)
                settle(pool)
                pool.indirect_dma_start(out=out_rows[:, :],
                                        out_offset=bass.IndirectOffsetOnAxis(ap=sidx[:, q:q + 1], axis=0),
                                        in_=res[q][:, :], in_offset=None, compute_op=ALU.add).then_inc(s_sc, 16)
                pool.wait_ge(s_sc, slot * 16 + 16)
                pool.sem_inc(s_resf, 1)

            n = slots(pool, step)
            pool.wait_ge(s_sc, n * 16)
            pool.wait_ge(s_g[0], ((n + 3) >> 1) * 16)
            pool.wait_ge(s_g[1], ((n + 2) >> 1) * 16)

        @block.scalar
        def _(act):
            act.wait_ge(s_par, 16 * 7)
            act.activation(drv[:, TX:TF + 1], par[:, 4:6], ACT.Tanh).then_inc(s_tanh, 1)
            act.wait_ge(s_drv, 1)

            def quantise_ctx(k):
                act.wait_ge(s_ctx[k % CB], 16 * (k // CB + 1))
                if k >= 2:
                    act.wait_ge(s_q2, k - 1)
                act.activation(u8c[:, k % 2, :], stage[:, k % CB, :], ACT.Identity, scale=dv(INV2),
                               bias=par[:, 3:4]).then_inc(s_uc, 1)

            def std(which, i):
                act.wait_ge(s_var[which], i + 1)
                act.activation(lnv[:, which, i, STD:STD + 1], lnv[:, which, i, VE:VE + 1], ACT.Sqrt).then_inc(s_std[which], 1)

            def quantise_x(i):
                act.wait_ge(s_ab[0], i + 1)
                if i >= 2:
                    act.wait_ge(s_q1, i - 1)
                act.activation(u8x[:, i % 2, :], xt[:, i, :], ACT.Identity, scale=lnv[:, 0, i, AA:AA + 1],
                               bias=lnv[:, 0, i, BB:BB + 1]).then_inc(s_u, 1)

            def keep_q1T(i):
                act.wait_ge(s_qt, i + 1)
                act.activation(q1T[:, i, :, :], ps_q[:, :, :], ACT.Copy).then_inc(s_qe, 1)

            def add_rowsum(i):
                act.wait_ge(s_sread, i + 1)
                act.activation(xt[:, i, :], xt[:, i, :], ACT.Identity, bias=rsum[:, i:i + 1]).then_inc(s_xr, 1)

            def make_corr(b):
                act.wait_ge(s_att, b * (TPB + 1) + 1)
                act.activation(corr[:, b, :], ps[(b * (TPB + 1)) % 2][:, :], ACT.Identity, scale=dv(C1D1),
                               bias=dv(C1KDD)).then_inc(s_corr, 1)

            def normalise(i):
                act.wait_ge(s_ab[1], i + 1)
                if i >= 2:
                    act.wait_ge(s_ys, 16 * (i - 1))
                    act.wait_ge(s_yt, i - 1)
                act.activation(y[i % 2][:, :], xt[:, i, :], ACT.Identity, scale=lnv[:, 1, i, AA:AA + 1],
                               bias=lnv[:, 1, i, BB:BB + 1]).then_inc(s_y, 1)
                if i >= 1:
                    act.wait_ge(s_oi, 16 * i)
                    act.wait_ge(s_ys, 16 * i)
                act.wait_ge(s_xn, i + 1)
                act.dma_start(out_t[i], xt[:, i, :]).then_inc(s_oi, 16)
                act.wait_ge(s_y, i + 1)
                act.dma_start(y_t[i], y[i % 2][:, :]).then_inc(s_ys, 16)

            def keep_yT(i):
                act.wait_ge(s_yt, i + 1)
                if i >= 2:
                    act.wait_ge(s_small, i + 1)
                act.activation(yT[i % 2][:, :, :], ps_y[:, :, :], ACT.Copy).then_inc(s_ye, 1)

            def split_hi0(c):
                act.wait_ge(s_w[c], 16)
                if c == NCH // 2:
                    act.wait_ge(s_att, NT + B)
                act.activation(w_hi[:, c * CW:(c + 1) * CW], stage[:, CK * c:CK * (c + 1), :].rearrange("p k h -> p (k h)"),
                               ACT.Copy).then_inc(s_hi, 1)

            quantise_ctx(0)
            std(0, 0)
            quantise_ctx(1)
            quantise_x(0)
            std(0, 1)
            quantise_ctx(2)
            quantise_x(1)
            std(0, 2)
            quantise_ctx(3)
            quantise_x(2)
            std(0, 3)
            quantise_ctx(4)
            keep_q1T(0)
            quantise_ctx(5)
            quantise_x(3)
            keep_q1T(1)
            quantise_ctx(6)
            keep_q1T(2)
            quantise_ctx(7)
            keep_q1T(3)
            add_rowsum(0)
            make_corr(0)
            for i in range(NT + 2):
                if i < TPB:
                    quantise_ctx(KT + 2 * i)
                    quantise_ctx(KT + 2 * i + 1)
                if i == TPB:
                    make_corr(1)
                if i < NT:
                    std(1, i)
                if i < TPB:
                    std(0, i + TPB)
                if i + 1 < NT:
                    add_rowsum(i + 1)
                if 1 <= i <= NT:
                    keep_yT(i - 1)
                if i < NT:
                    normalise(i)
                if i < TPB:
                    quantise_x(i + TPB)
                if 2 <= i < NT - 2:
                    keep_q1T(i + 2)
                if i == NT:
                    split_hi0(0)
                    split_hi0(1)
            split_hi0(2)
            split_hi0(3)

            def evacuate_hi(slot, q):
                act.activation(yT_hi[q][:, :, :], ps_y[:, :, :], ACT.Copy).then_inc(s_eh, 1)

            act.wait_ge(s_tab, 1)
            act.wait_ge(s_tp, 1)
            evacuate_hi(0, 0)
            act.wait_ge(s_oi, 16 * NT)

            def step(slot, q, turn):
                act.wait_ge(s_tp, slot + 2)
                act.wait_ge(s_mm, slot + 1)
                evacuate_hi(slot + 1, 1 - q)
                nxt = entry(act, NXT, slot, E - 1)
                with act.If(nxt > 0):
                    dst = act.snap((nxt & 1) * WSZ)
                    for c in range(NCH):
                        act.wait_ge(s_w[c], nxt * 16 + 16)
                        act.activation(w_hi[:, bass.ds(dst + c * CW, CW)],
                                       stage[:, CK * c:CK * (c + 1), :].rearrange("p k h -> p (k h)"),
                                       ACT.Copy).then_inc(s_hi, 1)
                act.nop()

            slots(act, step)

        @block.vector
        def _(dve):
            n_steps = [0]

            def link(ins):
                n_steps[0] += 1
                ins.then_inc(s_v, 1)
                dve.wait_ge(s_v, n_steps[0])

            dve.sem_inc(s_free, 2)
            dve.wait_ge(s_par, 16 * 7)
            dve.reciprocal(dv(INV1), par[:, 0:1])
            dve.reciprocal(dv(INV2), par[:, 2:3])
            dve.tensor_scalar(dv(D1), par[:, 1:2], -1.0, QMID, ALU.mult, ALU.add)
            link(dve.tensor_scalar(dv(D2), par[:, 3:4], -1.0, QMID, ALU.mult, ALU.add))
            dve.wait_ge(s_tanh, 1)
            link(dve.tensor_scalar(dv(C1), dv(TX), par[:, 0:1], par[:, 2:3], ALU.mult, ALU.mult))
            dve.tensor_scalar(dv(C2), dv(TF), 1.0 / TOPK, None, ALU.mult)
            dve.tensor_scalar(dv(C1D1), dv(C1), dv(D1), None, ALU.mult)
            link(dve.tensor_scalar(dv(C1D2), dv(C1), dv(D2), None, ALU.mult))
            dve.tensor_scalar(dv(C1KDD), dv(C1D1), dv(D2), float(D), ALU.mult, ALU.mult).then_inc(s_drv, 1)
            dve.wait_ge(s_drv, 1)
            dve.wait_ge(s_const, 1)

            def ln(which, i, c):
                return lnv[:, which, i, c:c + 1]

            def stats(which, i):
                for h in range(HB):
                    last = dve.bn_stats(st[:, which, h, :], xt[:, i, h * 512:(h + 1) * 512])
                link(last)
                link(dve.bn_aggr(mv[:, which, i, :], st[:, which, :, :].rearrange("p a b -> p (a b)")))
                dve.tensor_scalar(ln(which, i, VE), mv[:, which, i, 1:2], EPS, None, ALU.add).then_inc(s_var[which], 1)

            def scales(which, i):
                dve.wait_ge(s_var[which], i + 1)
                dve.wait_ge(s_std[which], i + 1)
                link(dve.reciprocal(ln(which, i, RST), ln(which, i, STD)))
                link(dve.tensor_scalar(ln(which, i, T1), ln(which, i, RST), ln(which, i, RST), ln(which, i, VE), ALU.mult, ALU.mult))
                link(dve.tensor_scalar(ln(which, i, T2), ln(which, i, T1), 0.5, -1.5, ALU.mult, ALU.add))
                if which == 0:
                    link(dve.tensor_scalar(ln(which, i, NA), ln(which, i, T2), ln(which, i, RST), dv(INV1), ALU.mult, ALU.mult))
                    dve.tensor_scalar(ln(which, i, BB), mv[:, which, i, 0:1], ln(which, i, NA), par[:, 1:2], ALU.mult, ALU.add)
                else:
                    link(dve.tensor_scalar(ln(which, i, NA), ln(which, i, T2), ln(which, i, RST), None, ALU.mult))
                    dve.tensor_scalar(ln(which, i, BB), mv[:, which, i, 0:1], ln(which, i, NA), None, ALU.mult)
                dve.tensor_scalar(ln(which, i, AA), ln(which, i, NA), -1.0, None, ALU.mult).then_inc(s_ab[which], 1)

            def centre_x(i):
                dve.wait_ge(s_u, i + 1)
                if i >= 2:
                    dve.wait_ge(s_qt, i - 1)
                dve.tensor_scalar(q1[:, i % 2, :], u8x[:, i % 2, :], 1.0, -QMID, ALU.mult, ALU.add).then_inc(s_q1, 1)

            def x_new(i):
                dve.wait_ge(s_att, i + 2 + i // TPB)
                dve.wait_ge(s_xc, i + 1)
                dve.scalar_tensor_tensor(xt[:, i, :], ps[(i + 1 + i // TPB) % 2][:, :], dv(C1), xt[:, i, :],
                                         ALU.mult, ALU.add).then_inc(s_xn, 1)
                dve.wait_ge(s_xn, i + 1)

            def select(i):
                link(dve.tensor_tensor(lg[:, :], ps_s[:, GT_C:GT_C + E], bg[:, :], ALU.add))
                other = lg[:, :].unsqueeze(1).to_broadcast([P, E, E])
                own = lg[:, :].unsqueeze(2).to_broadcast([P, E, E])
                dve.tensor_tensor(pw[:, 0], other, own, ALU.is_gt)
                link(dve.tensor_tensor(pw[:, 1], other, own, ALU.is_equal))
                link(dve.tensor_tensor(pw[:, 2], pw[:, 1], tri[:, 0:E, :], ALU.mult))
                link(dve.tensor_tensor(pw[:, 3], pw[:, 2], pw[:, 0], ALU.add))
                link(dve.tensor_reduce(rank[:, :], pw[:, 3], axis=AX.X, op=ALU.add))
                link(dve.tensor_scalar(sel[:, i, :], rank[:, :], float(TOPK), None, ALU.is_lt))
                dve.tensor_tensor(run[:, i + 1, :], run[:, i, :], sel[:, i, :], ALU.add)
                dve.tensor_scalar(sgn[:, i, :], sel[:, i, :], tok1m2[:, i:i + 1], tok1[:, i:i + 1],
                                  ALU.mult, ALU.add).then_inc(s_sel, 1)
                dve.wait_ge(s_sel, i + 1)

            def positions(i):
                link(dve.scalar_tensor_tensor(pos[:, :], sel[:, i, :], backm[:, i:i + 1], ps_s[:, CU_C:CU_C + E],
                                              ALU.mult, ALU.add))
                link(dve.tensor_scalar(pos[:, :], pos[:, :], back[:, i:i + 1], None, ALU.add))
                link(dve.tensor_scalar(pHi[:, :], pos[:, :], 1.0 / P, -0.498, ALU.mult, ALU.add))
                link(dve.tensor_copy(pH[:, i, :], pHi[:, :]))
                link(dve.scalar_tensor_tensor(pL[:, i, :], pH[:, i, :], -float(P), pos[:, :], ALU.mult, ALU.add))
                dve.wait_ge(s_oi, 16 * (i + 1))
                dve.wait_ge(s_y, i + 1)
                dve.tensor_tensor(onehot[i][:, :, :], pL[:, i, :].unsqueeze(2).to_broadcast([P, E, P]),
                                  iota_b[:, :].unsqueeze(1).to_broadcast([P, E, P]), ALU.is_equal).then_inc(s_oh, 1)

            def small(i):
                dve.wait_ge(s_small, i + 2)
                if i + 1 < NT:
                    link(dve.tensor_scalar(rsum[:, i + 1:i + 2], ps_s[:, RS_C:RS_C + 1], dv(C1D2), None, ALU.mult))
                if 2 <= i < NT + 2:
                    select(i - 2)
                if i >= 3:
                    positions(i - 3)
                if i < NT + 2:
                    dve.nop().then_inc(s_sread, 1)

            for i in range(TPB):
                dve.wait_ge(s_x[i], 16)
                stats(0, i)
                if i >= 1:
                    scales(0, i - 1)
                if i >= 2:
                    centre_x(i - 2)
            scales(0, TPB - 1)
            centre_x(TPB - 2)
            centre_x(TPB - 1)
            small(-1)
            for i in range(NT + 3):
                if i < NT:
                    x_new(i)
                    stats(1, i)
                if i < TPB:
                    dve.wait_ge(s_x[i + TPB], 16)
                    stats(0, i + TPB)
                small(i)
                if i < NT:
                    scales(1, i)
                if i < TPB:
                    scales(0, i + TPB)
                if 1 <= i <= TPB:
                    centre_x(i + TPB - 1)

            count, base_ = cnt[:, 0, 0:E], cnt[:, 1, :]
            link(dve.tensor_scalar(cnt8[:, :], ps_s[:, TO_C:TO_C + E], 1.0 / P, 0.494, ALU.mult, ALU.add))
            link(dve.tensor_scalar(count, cnt8[:, :], 1.0, None, ALU.max))
            link(dve.tensor_tensor(tri9[:, :, :], tri[:, :, :], count.unsqueeze(1).to_broadcast([P, E + 1, E]), ALU.mult))
            link(dve.tensor_reduce(base_, tri9[:, :, :], axis=AX.X, op=ALU.add))
            link(dve.tensor_tensor(sid[:, :, :], pH[:, :, :], count.unsqueeze(1).to_broadcast([P, NT, E]), ALU.is_ge))
            link(dve.scalar_tensor_tensor(sid[:, :, :], sid[:, :, :], 1000.0, pH[:, :, :], ALU.mult, ALU.add))
            link(dve.tensor_tensor(sid[:, :, :], sid[:, :, :], base_[:, 0:E].unsqueeze(1).to_broadcast([P, NT, E]), ALU.add))
            te = NT * E
            flat = lambda a: a.rearrange("p i e -> p (i e)").unsqueeze(2).to_broadcast([P, te, NS])
            link(dve.tensor_tensor(cmp.ap().rearrange("p i e s -> p (i e) s"), flat(sid[:, :, :]),
                                   iota_f[:, 0:NS].unsqueeze(1).to_broadcast([P, te, NS]), ALU.is_equal))
            dve.tensor_tensor(R.ap().rearrange("p i e s -> p (i e) s"), cmp.ap().rearrange("p i e s -> p (i e) s"),
                              flat(sgn[:, :, :]), ALU.mult).then_inc(s_R, 1)
            slot_no = iota_f[:, 0:NS].unsqueeze(2).to_broadcast([P, NS, E - 1])
            ends = base_[:, 1:E].unsqueeze(1).to_broadcast([P, NS, E - 1])
            starts = base_[:, 0:E - 1].unsqueeze(1).to_broadcast([P, NS, E - 1])
            s7 = sc26[:, :, 0:E - 1]
            link(dve.tensor_tensor(s7, slot_no, ends, ALU.is_ge))
            link(dve.tensor_reduce(sv[:, 0, :], s7, axis=AX.X, op=ALU.add))
            link(dve.tensor_tensor(s7, slot_no, starts, ALU.is_equal))
            link(dve.tensor_tensor(s7, s7, iota_f[:, 1:E].unsqueeze(1).to_broadcast([P, NS, E - 1]), ALU.mult))
            link(dve.tensor_reduce(sv[:, 1, :], s7, axis=AX.X, op=ALU.add))
            link(dve.tensor_scalar(svi[:, :], sv[:, 0, :], 0.5, -0.25, ALU.mult, ALU.add))
            link(dve.tensor_copy(sv[:, 2, :], svi[:, :]))
            link(dve.scalar_tensor_tensor(sv[:, 3, :], sv[:, 2, :], -2.0, sv[:, 0, :], ALU.mult, ALU.add))
            dve.tensor_scalar(tab[:, NEED:NEED + NS], sv[:, 0, :], float(NCH), float(NCH), ALU.mult, ALU.add)
            dve.tensor_scalar(tab[:, WOFF:WOFF + NS], sv[:, 3, :], float(WSZ), None, ALU.mult)
            dve.tensor_copy(tab[:, NXT:NXT + NS], sv[:, 1, :])
            dve.tensor_copy(tab[:, BAS:BAS + E + 1], base_).then_inc(s_tab, 1)
            dve.wait_ge(s_idx_ps, 1)
            link(dve.tensor_copy(sv[:, 4, :], ps_s[:, 0:NS]))
            link(dve.scalar_tensor_tensor(sv[:, 5, :], sv[:, 4, :], -1.0, sv[:, 4, :], ALU.mult, ALU.max))
            dve.tensor_scalar(idx[:, :], sv[:, 5, :], 1.0, -1.0, ALU.max, ALU.add)
            dve.tensor_scalar(weight[:, :], ps_s[:, 0:NS], 0.0, dv(C2), ALU.is_lt, ALU.mult).then_inc(s_idx, 1)
            dve.wait_ge(s_idx, 1)
            dve.wait_ge(s_tab, 1)

            def evacuate_lo(q):
                dve.tensor_tensor(yT_lo[q][:, :, :], ps_y[:, :, :], yT_hi[q][:, :, :].bitcast(f32),
                                  ALU.subtract).then_inc(s_el, 1)

            dve.wait_ge(s_eh, 1)
            evacuate_lo(0)
            dve.wait_ge(s_oi, 16 * NT)

            def step(slot, q, turn):
                dve.wait_ge(s_eh, slot + 2)
                evacuate_lo(1 - q)
                nxt = entry(dve, NXT, slot, E - 1)
                with dve.If(nxt > 0):
                    dst = dve.snap((nxt & 1) * WSZ)
                    for c in range(NCH):
                        dve.wait_ge(s_hi, nxt * NCH + c + 1)
                        dve.tensor_tensor(w_lo[:, bass.ds(dst + c * CW, CW)],
                                          stage[:, CK * c:CK * (c + 1), :].rearrange("p k h -> p (k h)"),
                                          w_hi[:, bass.ds(dst + c * CW, CW)].bitcast(f32), ALU.subtract).then_inc(s_lo, 1)
                woff = entry(dve, WOFF, slot, WSZ)
                need = entry(dve, NEED, slot, NCH * E)
                for b in range(2):
                    with dve.If(woff == b * WSZ):
                        dve.wait_ge(s_bias[b], ((need + NCH) >> 3) * 16)
                        settle(dve)
                dve.wait_ge(s_mm, slot + 2)
                dve.wait_ge(s_resf, slot + 1)
                dve.tensor_tensor(res[q][:, :], ps[q][:, :], bias[:, bass.ds(woff >> 3, D)], ALU.add).then_inc(s_free, 1)
                dve.wait_ge(s_free, slot + 3)
                dve.tensor_scalar(res[q][:, :], res[q][:, :], 0.0, weight[:, bass.ds(slot, 1)],
                                  ALU.max, ALU.mult).then_inc(s_post, 1)

            slots(dve, step)

        @block.tensor
        def _(pe):
            pe.wait_ge(s_const, 1)

            def transpose_q1(i):
                pe.wait_ge(s_q1, i + 1)
                if i >= 1:
                    pe.wait_ge(s_qe, i)
                for k in range(KT):
                    last = pe.transpose(ps_q[:, k, :], q1[:, i % 2, k * P:(k + 1) * P], ident_b[:, :])
                last.then_inc(s_qt, 1)

            def column_sums(b):
                u = b * (TPB + 1)
                if u >= 2:
                    pe.wait_ge(s_xn, u - 2)
                for k in range(KT):
                    pe.wait_ge(s_q2, b * KT + k + 1)
                    for h in range(HB):
                        last = pe.matmul(ps[u % 2][:, h * 512:(h + 1) * 512], ones_b[:, :],
                                         q2[:, b * KT + k, h * 512:(h + 1) * 512], start=(k == 0), stop=(k == KT - 1))
                last.then_inc(s_att, 1)

            def attention(i):
                b = i // TPB
                u = i + 1 + b
                if u == 2 or u == TPB + 3:
                    pe.wait_ge(s_corr, b + 1)
                if i >= 2 and u != TPB + 3:
                    pe.wait_ge(s_xn, i - 1 if i != TPB else TPB)
                for k in range(KT):
                    for h in range(HB):
                        last = pe.matmul(ps[u % 2][:, h * 512:(h + 1) * 512], q1T[:, i, k, :],
                                         q2[:, b * KT + k, h * 512:(h + 1) * 512], start=(k == 0), stop=(k == KT - 1))
                last.then_inc(s_att, 1)

            def transpose_y(i):
                pe.wait_ge(s_y, i + 1)
                if i >= 1:
                    pe.wait_ge(s_ye, i)
                for k in range(KT):
                    last = pe.transpose(ps_y[:, k, :], y[i % 2][:, k * P:(k + 1) * P], ident_f[:, :])
                last.then_inc(s_yt, 1)

            def small(i):
                if i >= 0:
                    pe.wait_ge(s_sread, i + 1)
                if i + 1 < NT:
                    pe.wait_ge(s_qe, i + 2)
                    for k in range(KT):
                        last = pe.matmul(ps_s[:, RS_C:RS_C + 1], q1T[:, i + 1, k, :], ones_b[:, 0:1],
                                         start=(k == 0), stop=(k == KT - 1))
                if 2 <= i < NT + 2:
                    pe.wait_ge(s_ye, i - 1)
                    for k in range(KT):
                        last = pe.matmul(ps_s[:, GT_C:GT_C + E], yT[i % 2][:, k, :], wg[:, k, :],
                                         start=(k == 0), stop=(k == KT - 1))
                if i >= 3:
                    pe.wait_ge(s_sel, i - 2)
                    pe.matmul(ps_s[:, CU_C:CU_C + E], before[:, :], sel[:, i - 3, :], start=True, stop=False)
                    last = pe.matmul(ps_s[:, CU_C:CU_C + E], ones_b[:, :], run[:, i - 3, :], start=False, stop=True)
                if i == NT + 2:
                    last = pe.matmul(ps_s[:, TO_C:TO_C + E], ones_b[:, :], run[:, NT, :], start=True, stop=True)
                last.then_inc(s_small, 1)

            for i in range(TPB):
                transpose_q1(i)
            small(-1)
            pe.wait_ge(s_wg, 16)
            column_sums(0)
            for i in range(NT + 3):
                if i == TPB:
                    column_sums(1)
                if i < NT:
                    attention(i)
                small(i)
                if 2 <= i < NT - 2:
                    transpose_q1(i + 2)
                if 1 <= i <= NT:
                    transpose_y(i - 1)
            pe.wait_ge(s_R, 1)
            for i in range(NT):
                pe.wait_ge(s_oh, i + 1)
                for e in range(E):
                    last = pe.matmul(ps_s[:, 0:NS], onehot[i][:, e, :], R[:, i, e, :],
                                     start=(i == 0 and e == 0), stop=(i == NT - 1 and e == E - 1))
            last.then_inc(s_idx_ps, 1)

            def transpose_slot(q):
                for k in range(KT):
                    last = pe.transpose(ps_y[:, k, :], y_rows[q][:, k * P:(k + 1) * P], ident_f[:, :])
                last.then_inc(s_tp, 1)

            pe.wait_ge(s_tab, 1)
            pe.wait_ge(s_idx_ps, 1)
            pe.sem_inc(s_mm, 1)
            pe.wait_ge(s_g[0], 16)
            transpose_slot(0)

            def step(slot, q, turn):
                pe.wait_ge(s_g[1 - q], turn * 16 + (16 if q == 0 else 32))
                pe.wait_ge(s_el, slot + 1)
                transpose_slot(1 - q)
                pe.wait_ge(s_lo, entry(pe, NEED, slot, NCH * E))
                woff = entry(pe, WOFF, slot, WSZ)
                pe.wait_ge(s_free, slot + 1)
                for k in range(KT):
                    for lhs, w in ((yT_hi, w_hi), (yT_hi, w_lo), (yT_lo, w_hi)):
                        for h in range(HB):
                            last = pe.matmul(ps[q][:, h * 512:(h + 1) * 512], lhs[q][:, k, :],
                                             w[:, bass.ds(woff + k * D + h * 512, 512)],
                                             start=(k == 0 and lhs is yT_hi and w is w_hi),
                                             stop=(k == KT - 1 and lhs is yT_lo))
                last.then_inc(s_mm, 1)

            slots(pe, step)


_INS = ["x", "ctx_4096", "g_xattn", "g_ffn", "L0_xattn_x1_scale", "L0_xattn_x1_zp", "L0_xattn_x2_scale",
        "L0_xattn_x2_zp", "L0_ffn_W_gate", "L0_ffn_b_gate", "L0_ffn_W_e", "L0_ffn_b_e"]
_OUTS = [((2, 512, 1024), "float32")]


def kernel(**inputs):
    import numpy as _np
    import concourse.bacc as _bacc
    from concourse import mybir as _mybir
    from concourse.bass_utils import run_bass_kernel_spmd as _run

    nc = _bacc.Bacc("TRN2", target_bir_lowering=False, num_devices=1)
    arrays, args = {}, []
    for name in _INS:
        a = _np.ascontiguousarray(inputs[name])
        arrays[f"in_{name}_dram"] = a
        args.append(nc.dram_tensor(f"in_{name}_dram", a.shape, _mybir.dt.from_np(a.dtype), kind="ExternalInput").ap())
    for i, (shape, dtype) in enumerate(_OUTS):
        dt = _mybir.dt.from_np(_np.dtype(dtype))
        args.append(nc.dram_tensor(f"out_{i}_dram", shape, dt, kind="ExternalOutput").ap())
    flamingo_gated_moe(nc, *args)
    r = _run(nc, [arrays], core_ids=[0])
    got = tuple(r.results[0][f"out_{i}_dram"] for i in range(len(_OUTS)))
    return got[0]
```

```python
import concourse.bass as bass
from concourse import mybir
from contextlib import ExitStack


def flamingo_gated_moe(nc, x, ctx_kv, g_xattn, g_ffn, x1_scale, x1_zp, x2_scale, x2_zp,
                       W_gate, b_gate, W_e, b_e, out):
    f32, f32r, bf16, f16 = mybir.dt.float32, mybir.dt.float32r, mybir.dt.bfloat16, mybir.dt.float16
    i32, u32, u8 = mybir.dt.int32, mybir.dt.uint32, mybir.dt.uint8
    ALU, ACT = mybir.AluOpType, mybir.ActivationFunctionType
    AX = mybir.AxisListType

    P = 128
    B, S, D = x.shape
    E = W_e.shape[0]
    KT = D // P
    NT = B * S // P
    TPB = S // P
    HB = D // 512
    TOPK = 2
    MAX_SLOTS = (TOPK * NT * P - E) // P + E
    NS = MAX_SLOTS + 4
    QMID = 128.0
    EPS = 1e-5
    WSZ = KT * D
    NCH = 4
    CK = KT // NCH
    CW = WSZ // NCH
    NLO = NCH - 1

    x_t = x.rearrange("b (n p) d -> (b n) p d", p=P)
    out_rows = out.rearrange("b s d -> (b s) d")
    out_t = out.rearrange("b (n p) d -> (b n) p d", p=P)
    ctx_t = ctx_kv.rearrange("b (k p) d -> (b k) p d", p=P)
    w_t = W_e.rearrange("e (k p) h -> p e k h", p=P)
    y_dram = nc.dram_tensor("y_scratch", (NT * P, D), f32, kind="Internal").ap()
    y_t = y_dram.rearrange("(n p) d -> n p d", p=P)

    ctx = ExitStack()
    with ctx:
        def sb(name, shape, dt):
            return ctx.enter_context(nc.sbuf_tensor(name, shape, dt))

        def sem(name):
            return ctx.enter_context(nc.semaphore(name))

        KB = 1024
        arena = sb("arena", [P, 200 * KB], u8)
        base = nc.sbuf_base - 200 * KB

        def at(name, shape, dt, off):
            return nc.alloc_sbuf_tensor_at(name, shape, dt, offset=base + off)

        WHI, WLO, STG, YT, GB, RES, BIA = 0, 64 * KB, 128 * KB, 160 * KB, 176 * KB, 184 * KB, 192 * KB
        w_hi = at("w_hi", [P, 2 * WSZ], f32r, WHI)
        w_lo = at("w_lo", [P, 2 * WSZ], f32r, WLO)
        stage = at("stage", [P, KT, D], f32, STG)
        yT_hi = [at(f"yT_hi{q}", [P, KT, P], f32r, YT + 4 * KB * q) for q in range(2)]
        yT_lo = [at(f"yT_lo{q}", [P, KT, P], f32r, YT + 8 * KB + 4 * KB * q) for q in range(2)]
        y_rows = [at(f"y_rows{q}", [P, D], f32, GB + 4 * KB * q) for q in range(2)]
        res = [at(f"res{q}", [P, D], f32, RES + 4 * KB * q) for q in range(2)]
        bias = at("bias", [P, 2 * D], f32, BIA)
        xt = at("xt", [P, NT, D], f32, WHI + 32 * KB)
        q1T = at("q1T", [P, NT, KT, P], bf16, WLO)
        onehot = [at(f"onehot{i}", [P, P, E], bf16, WLO + 2 * KB * i) for i in range(NT)]
        q2 = at("q2", [P, B * KT, D], bf16, WLO + 32 * KB)
        q1 = at("q1", [P, 2, D], bf16, RES)
        yT = [at(f"yT{q}", [P, KT, P], f32, YT + 4 * KB * q) for q in range(2)]
        y = [at(f"y{q}", [P, D], f32, GB + 4 * KB * q) for q in range(2)]
        CB = 6
        corr = stage[:, CB:CB + B, :]
        u8x = sb("u8x", [P, 2, D], u8)
        u8c = at("u8c", [P, 2, D], u8, RES + 4 * KB)

        ident_b = sb("ident_b", [P, P], bf16)
        ident_f = sb("ident_f", [P, P], f32)
        ones_b = at("ones_b", [P, P], bf16, YT + 8 * KB)
        before = at("before", [P, P], bf16, YT + 8 * KB + 256)
        iota_f = at("iota_f", [P, 32], f32, YT + 8 * KB + 512)
        wg = at("wg", [P, KT, E], f32, YT + 10 * KB)
        tri = at("tri", [P, E + 1, E], f32, YT + 10 * KB + 256)
        iota_pe = at("iota_pe", [P, P, E], bf16, WLO + 16 * KB)
        iota_se = at("iota_se", [P, NS, NT, E], f16, WLO + 18 * KB)
        cmp = at("cmp", [P, NS, NT, E], f16, WLO + 22 * KB)
        R = at("R", [P, NS, NT, E], f16, WLO + 26 * KB)
        tok1 = sb("tok1", [P, NT], f32)
        back = sb("back", [P, NT], f32)
        par = sb("par", [P, 6], f32)
        bg = sb("bg", [P, E], f32)
        drv = sb("drv", [P, 16], f32)
        INV1, INV2, D1, D2, C1, C1D1, C1D2, C1KDD, C2, TX, TF, TMP = range(12)

        def dv(c):
            return drv[:, c:c + 1]

        eps = sb("eps", [P, 1], f32)
        st = sb("st", [P, 2, HB, 6], f32)
        mv = sb("mv", [P, 2, NT, 2], f32)
        lnv = sb("lnv", [P, 2, 6, NT], f32)
        STD, RST, T1, T2, AA, BB = range(6)
        rsum = sb("rsum", [P, NT], f32)
        lg = sb("lg", [P, TPB, E], f32)
        pw = at("pw", [P, 4, TPB, E, E], bf16, WLO + 30 * KB)
        rank = sb("rank", [P, TPB, E], f32)
        sel = sb("sel", [P, NT + 1, E], bf16)
        flip = sb("flip", [P, TPB, E], f32)
        sgn = sb("sgn", [P, NT, E], f16)
        nback = sb("nback", [P, TPB, E], f32)
        pos = sb("pos", [P, TPB, E], f32)
        pH = sb("pH", [P, NT, E], u8)
        pL = sb("pL", [P, NT, E], bf16)
        cnt = sb("cnt", [P, 6, 9], f32)
        cnt8 = sb("cnt8", [P, E], u8)
        tri9 = sb("tri9", [P, E + 1, E], f32)
        sid = sb("sid", [P, NT, E], f32)
        sid_h = sb("sid_h", [P, NT, E], f16)
        sc26 = at("sc26", [P, NS, E], f32, RES + 7 * KB)
        sv = at("sv", [P, 6, NS], f32, RES + 5 * KB)
        svi = sb("svi", [P, NS], u8)
        tab = sb("tab", [P, 3 * NS + E + 1], i32)
        NEED, WOFF, NXT, BAS = 0, NS, 2 * NS, 3 * NS
        idx = sb("idx", [P, NS], u32)
        weight = sb("weight", [P, NS], f32)
        gidx = sb("gidx", [P, 2], u32)
        sidx = sb("sidx", [P, 2], u32)

        ps = [ctx.enter_context(nc.psum_tensor(f"ps{i}", [P, HB * 512], f32)) for i in range(2)]
        ps_q = ctx.enter_context(nc.psum_tensor("ps_q", [P, KT, P], bf16))
        ps_y = ctx.enter_context(nc.psum_tensor("ps_y", [P, KT, P], f32))
        ps_s = ctx.enter_context(nc.psum_tensor("ps_s", [P, 512], f32))
        RS_C, GT_C, CU_C = 0, NT, NT + NT * E

        s_par = sem("params_landed")
        s_wg = sem("gate_landed")
        s_x = [sem(f"x_landed{i}") for i in range(NT)]
        s_ctx = [sem(f"ctx_landed{i}") for i in range(CB)]
        s_w = [sem(f"w_landed{c}") for c in range(NCH)]
        s_bias = [sem(f"bias_landed{q}") for q in range(2)]
        s_const = sem("consts_made")
        s_cstep = sem("const_step")
        s_tanh = sem("tanh_done")
        s_drv = sem("params_derived")
        s_v = sem("dve_step")
        s_var = [sem("var1_ready"), sem("var2_ready")]
        s_std = [sem("std1_ready"), sem("std2_ready")]
        s_ab = [sem("scale1_ready"), sem("scale2_ready")]
        s_q1 = sem("q1_ready")
        s_qt = sem("q1T_in_psum")
        s_qe = sem("q1T_ready")
        s_uc = sem("ctx_quantised")
        s_q2 = sem("q2_ready")
        s_att = sem("attn_in_psum")
        s_small = sem("small_in_psum")
        s_sread = sem("small_read")
        s_corr = sem("corr_ready")
        s_xc = sem("x_plus_corr")
        s_xn = sem("x_new_ready")
        s_y = sem("y_ready")
        s_oa = sem("x_new_with_rowsum")
        s_rs = sem("rowsums_ready")
        s_oi = sem("x_new_stored")
        s_ys = [sem(f"y_stored{q}") for q in range(2)]
        s_yt = sem("yT_in_psum")
        s_ye = sem("yT_ready")
        s_sel = sem("selection_ready")
        s_oh = sem("onehots_ready")
        s_R = sem("slot_matrix_ready")
        s_idx_ps = sem("indices_in_psum")
        s_idx = sem("indices_ready")
        s_tab = sem("schedule_ready")
        s_hi = sem("w_hi_done")
        s_lo = sem("w_lo_done")
        s_lop = sem("w_lo_last_done")
        s_pool = sem("pool_step")
        s_g = [sem(f"gathered{q}") for q in range(2)]
        s_tp = sem("slot_yT_in_psum")
        s_eh = sem("slot_yT_hi_ready")
        s_el = sem("slot_yT_lo_ready")
        s_mm = sem("slot_matmuls_done")
        s_free = sem("slot_psum_free")
        s_post = sem("slot_result_ready")
        s_resf = sem("slot_result_free")
        s_sc = sem("slot_scattered")
        s_settled = sem("waits_settled")

        block = ctx.enter_context(nc.Block())

        def slots(eng, body):
            n_used = eng.value_load(tab[0:1, BAS + E:BAS + E + 1], min_val=E, max_val=MAX_SLOTS)
            with eng.Fori(0, (MAX_SLOTS + 1) // 2) as turn:
                for q in range(2):
                    with eng.If(turn * 2 + q < n_used):
                        body(turn * 2 + q, q, turn)
            return n_used

        def entry(eng, field, slot, hi):
            return eng.value_load(tab[0:1, bass.ds(slot + field, 1)], min_val=0, max_val=hi)

        def settle(eng):
            eng.sem_inc(s_settled, 1)

        @block.sync
        def _(sp):
            def load_ctx(k):
                if k >= CB:
                    sp.wait_ge(s_uc, k - CB + 1)
                sp.dma_start(stage[:, k % CB, :], ctx_t[k]).then_inc(s_ctx[k % CB], 16)

            def load_x(i):
                sp.dma_start(xt[:, i, :], x_t[i]).then_inc(s_x[i], 16)

            for i in range(TPB):
                load_x(i)
                load_ctx(i)
            for k in range(TPB, KT):
                load_ctx(k)
            for i in range(TPB):
                load_x(TPB + i)
                load_ctx(KT + i)
            sp.dma_start(wg[:, :, :], W_gate.rearrange("(k p) e -> p k e", p=P)).then_inc(s_wg, 16)
            for k in range(KT + TPB, 2 * KT):
                load_ctx(k)

            def store_x_new(i):
                sp.wait_ge(s_oa, i + 1)
                sp.dma_start(out_t[i], xt[:, i, :]).then_inc(s_oi, 16)

            sp.wait_ge(s_uc, B * KT)
            for c in range(NLO):
                sp.dma_start(stage[:, CK * c:CK * (c + 1), :], w_t[:, 0, CK * c:CK * (c + 1), :]).then_inc(s_w[c], 16)
            for e in range(2):
                sp.dma_start(bias[:, e * D:(e + 1) * D], b_e[e].partition_broadcast(P)).then_inc(s_bias[e], 16)
            for i in range(TPB):
                store_x_new(i)
            sp.wait_ge(s_xc, NT)
            sp.dma_start(stage[:, CK * NLO:, :], w_t[:, 0, CK * NLO:, :]).then_inc(s_w[NLO], 16)
            for i in range(TPB, NT):
                store_x_new(i)
            sp.wait_ge(s_g[1], 16)
            with sp.Fori(1, E) as n:
                for c in range(NCH):
                    sp.wait_ge(s_hi, n * NCH - NCH + c + 1)
                    settle(sp)
                    if c < NLO:
                        sp.wait_ge(s_lo, n * NLO - NLO + c + 1)
                    else:
                        sp.wait_ge(s_lop, n)
                    sp.dma_start(stage[:, CK * c:CK * (c + 1), :],
                                 w_t[:, bass.ds(n, 1), CK * c:CK * (c + 1), :].rearrange("p e k h -> p (e k) h")
                                 ).then_inc(s_w[c], 16)
                with sp.If(n > 1):
                    sp.wait_ge(s_post, entry(sp, BAS - 1, n, MAX_SLOTS))
                    settle(sp)
                    for q in range(2):
                        with sp.If((n & 1) == q):
                            sp.dma_start(bias[:, q * D:(q + 1) * D],
                                         b_e[bass.ds(n, 1), :].rearrange("a d -> (a d)").partition_broadcast(P)
                                         ).then_inc(s_bias[q], 16)
                    sp.nop()
                sp.nop()

        @block.gpsimd
        def _(pool):
            pool.memset(ident_b[:, :], 0.0)
            pool.memset(ident_f[:, :], 0.0)
            pool.memset(ones_b[:, :], 1.0)
            pool.memset(before[:, :], 1.0)
            pool.memset(tri[:, :, :], 1.0)
            pool.memset(eps[:, :], EPS)
            pool.memset(sel[:, NT, :], 0.0)
            pool.iota(iota_f[:, :], [[1, 32]], base=0, channel_multiplier=0, allow_small_or_imprecise_dtypes=True)
            pool.iota(tok1[:, :], [[P, NT]], base=1, channel_multiplier=1, allow_small_or_imprecise_dtypes=True)
            pool.iota(back[:, :], [[-P, NT]], base=NT * P - 1, channel_multiplier=-1,
                      allow_small_or_imprecise_dtypes=True)
            pool.iota(iota_pe[:, :, :], [[1, P], [0, E]], base=0, channel_multiplier=0, allow_small_or_imprecise_dtypes=True)
            pool.iota(iota_se[:, :, :, :], [[1, NS], [0, NT * E]], base=0, channel_multiplier=0,
                      allow_small_or_imprecise_dtypes=True).then_inc(s_cstep, 1)
            pool.wait_ge(s_cstep, 1)
            pool.affine_select(out=ident_b[:, :], in_=ident_b[:, :], compare_op=ALU.not_equal, fill=1.0,
                               base=0, pattern=[[-1, P]], channel_multiplier=1)
            pool.affine_select(out=ident_f[:, :], in_=ident_f[:, :], compare_op=ALU.not_equal, fill=1.0,
                               base=0, pattern=[[-1, P]], channel_multiplier=1)
            pool.affine_select(out=before[:, :], in_=before[:, :], compare_op=ALU.is_gt, fill=0.0,
                               base=0, pattern=[[1, P]], channel_multiplier=-1)
            pool.affine_select(out=tri[:, :, :], in_=tri[:, :, :], compare_op=ALU.is_gt, fill=0.0,
                               base=0, pattern=[[1, E + 1], [-1, E]], channel_multiplier=0).then_inc(s_const, 1)
            pool.sem_inc(s_resf, 2)

            def centre_ctx(k):
                pool.wait_ge(s_uc, k + 1)
                pool.tensor_scalar(q2[:, k, :], u8c[:, k % 2, :], 1.0, -QMID, ALU.mult, ALU.add).then_inc(s_q2, 1)

            def add_corr(i):
                pool.wait_ge(s_corr, i // TPB + 1)
                if i in (0, TPB):
                    pool.wait_ge(s_q1, i + TPB)
                pool.tensor_tensor(xt[:, i, :], xt[:, i, :], corr[:, i // TPB, :], ALU.add).then_inc(s_xc, 1)

            def add_rowsum(i):
                if i % TPB == 0:
                    pool.wait_ge(s_rs, i // TPB + 1)
                pool.wait_ge(s_y, i + 1)
                pool.tensor_scalar(xt[:, i, :], xt[:, i, :], 1.0, rsum[:, i:i + 1], ALU.mult, ALU.add).then_inc(s_oa, 1)

            for k in range(KT + 1):
                centre_ctx(k)
            add_corr(0)
            centre_ctx(KT + 1)
            for i in range(1, NT):
                add_corr(i)
                if i <= 3:
                    centre_ctx(KT + 2 * i)
                    centre_ctx(KT + 2 * i + 1)
                if i >= TPB:
                    add_rowsum(i - TPB)
            for i in range(NT - TPB, NT):
                add_rowsum(i)

            def gather(slot, q, step):
                pool.tensor_copy(gidx[:, q:q + 1], idx[:, bass.ds(slot, 1)]).then_inc(s_pool, 1)
                pool.wait_ge(s_pool, step)
                settle(pool)
                pool.indirect_dma_start(out=y_rows[q][:, :], out_offset=None, in_=y_dram[:, :],
                                        in_offset=bass.IndirectOffsetOnAxis(ap=gidx[:, q:q + 1], axis=0)
                                        ).then_inc(s_g[q], 16)

            pool.wait_ge(s_idx, 1)
            pool.wait_ge(s_tab, 1)
            for q in range(2):
                pool.wait_ge(s_ys[q], 16 * NT // 2)
            pool.wait_ge(s_oi, 16 * NT)
            for q in range(2):
                gather(q, q, q + 1)

            def split_lo_last(chunk_no, dst):
                pool.wait_ge(s_hi, chunk_no)
                pool.tensor_tensor(w_lo[:, dst], stage[:, CK * NLO:, :].rearrange("p k h -> p (k h)"),
                                   w_hi[:, dst].bitcast(f32), ALU.subtract).then_inc(s_lop, 1)

            split_lo_last(NCH, slice(NLO * CW, NCH * CW))
            pool.wait_ge(s_tp, 1)
            gather(2, 0, 3)

            def step(slot, q, turn):
                pool.wait_ge(s_tp, slot + 2)
                gather(slot + 3, 1 - q, slot * 2 + 4)
                nxt = entry(pool, NXT, slot, E - 1)
                with pool.If(nxt > 0):
                    split_lo_last(nxt * NCH + NCH, bass.ds((nxt & 1) * WSZ + NLO * CW, CW))
                pool.tensor_copy(sidx[:, q:q + 1], idx[:, bass.ds(slot, 1)]).then_inc(s_pool, 1)
                pool.wait_ge(s_pool, slot * 2 + 5)
                pool.wait_ge(s_post, slot + 1)
                settle(pool)
                pool.indirect_dma_start(out=out_rows[:, :],
                                        out_offset=bass.IndirectOffsetOnAxis(ap=sidx[:, q:q + 1], axis=0),
                                        in_=res[q][:, :], in_offset=None, compute_op=ALU.add).then_inc(s_sc, 16)
                pool.wait_ge(s_sc, slot * 16 + 16)
                pool.sem_inc(s_resf, 1)

            n = slots(pool, step)
            pool.wait_ge(s_sc, n * 16)
            pool.wait_ge(s_g[0], ((n + 4) >> 1) * 16)
            pool.wait_ge(s_g[1], ((n + 3) >> 1) * 16)

        @block.scalar
        def _(act):
            for c, src in enumerate((x1_scale, x1_zp, x2_scale, x2_zp, g_xattn, g_ffn)):
                act.dma_start(par[:, c:c + 1], src.partition_broadcast(P)).then_inc(s_par, 16)
            act.dma_start(bg[:, :], b_gate.partition_broadcast(P)).then_inc(s_par, 16)
            act.wait_ge(s_par, 16 * 7)
            act.activation(drv[:, TX:TF + 1], par[:, 4:6], ACT.Tanh).then_inc(s_tanh, 1)
            act.wait_ge(s_drv, 1)

            def quantise_ctx(k):
                act.wait_ge(s_ctx[k % CB], 16 * (k // CB + 1))
                if k >= 2:
                    act.wait_ge(s_q2, k - 1)
                act.activation(u8c[:, k % 2, :], stage[:, k % CB, :], ACT.Identity, scale=dv(INV2),
                               bias=par[:, 3:4]).then_inc(s_uc, 1)

            def std(which, i, n, count):
                act.wait_ge(s_var[which], count)
                act.activation(lnv[:, which, STD, i:i + n], mv[:, which, i:i + n, 1], ACT.Sqrt,
                               bias=eps[:, :]).then_inc(s_std[which], 1)

            def keep_q1T(i):
                act.wait_ge(s_qt, i + 1)
                act.activation(q1T[:, i, :, :], ps_q[:, :, :], ACT.Copy).then_inc(s_qe, 1)

            def make_corr(b):
                act.wait_ge(s_att, b * (TPB + 1) + 1)
                act.activation(corr[:, b, :], ps[(b * (TPB + 1)) % 2][:, :], ACT.Identity, scale=dv(C1D1),
                               bias=dv(C1KDD)).then_inc(s_corr, 1)

            def normalise(i):
                act.wait_ge(s_ab[1], i + 1)
                if i >= 2:
                    act.wait_ge(s_ys[i % 2], 16 * (i // 2))
                    act.wait_ge(s_yt, i - 1)
                act.activation(y[i % 2][:, :], xt[:, i, :], ACT.Identity, scale=lnv[:, 1, AA, i:i + 1],
                               bias=lnv[:, 1, BB, i:i + 1]).then_inc(s_y, 1)
                act.wait_ge(s_y, i + 1)
                act.dma_start(y_t[i], y[i % 2][:, :]).then_inc(s_ys[i % 2], 16)

            def keep_yT(i):
                act.wait_ge(s_yt, i + 1)
                if i >= 2:
                    act.wait_ge(s_small, i + 1)
                act.activation(yT[i % 2][:, :, :], ps_y[:, :, :], ACT.Copy).then_inc(s_ye, 1)

            def split_hi0(c):
                act.wait_ge(s_w[c], 16)
                act.activation(w_hi[:, c * CW:(c + 1) * CW], stage[:, CK * c:CK * (c + 1), :].rearrange("p k h -> p (k h)"),
                               ACT.Copy).then_inc(s_hi, 1)

            quantise_ctx(0)
            quantise_ctx(1)
            std(0, 0, 2, 1)
            quantise_ctx(2)
            quantise_ctx(3)
            keep_q1T(0)
            std(0, 2, 2, 2)
            quantise_ctx(4)
            keep_q1T(1)
            quantise_ctx(5)
            keep_q1T(2)
            quantise_ctx(6)
            keep_q1T(3)
            quantise_ctx(7)
            std(0, 4, 2, 3)
            quantise_ctx(KT)
            make_corr(0)
            quantise_ctx(KT + 1)
            for i in range(NT + 1):
                if i == TPB:
                    make_corr(1)
                if i < NT:
                    std(1, i, 1, i + 1)
                if i == 0:
                    std(0, 6, 2, 4)
                if 1 <= i:
                    keep_yT(i - 1)
                if i < NT:
                    normalise(i)
                if i <= 1:
                    keep_q1T(TPB + 2 * i)
                    keep_q1T(TPB + 2 * i + 1)
                if i <= 2:
                    quantise_ctx(KT + 2 * i + 2)
                    quantise_ctx(KT + 2 * i + 3)
                if i == NT - 1:
                    split_hi0(0)
            for c in range(1, NCH):
                split_hi0(c)

            def evacuate_hi(slot, q):
                act.activation(yT_hi[q][:, :, :], ps_y[:, :, :], ACT.Copy).then_inc(s_eh, 1)

            act.wait_ge(s_tab, 1)
            act.wait_ge(s_tp, 1)
            evacuate_hi(0, 0)
            act.wait_ge(s_oi, 16 * NT)

            def step(slot, q, turn):
                act.wait_ge(s_tp, slot + 2)
                act.wait_ge(s_mm, slot + 1)
                evacuate_hi(slot + 1, 1 - q)
                nxt = entry(act, NXT, slot, E - 1)
                with act.If(nxt > 0):
                    dst = act.snap((nxt & 1) * WSZ)
                    for c in range(NCH):
                        act.wait_ge(s_w[c], nxt * 16 + 16)
                        act.activation(w_hi[:, bass.ds(dst + c * CW, CW)],
                                       stage[:, CK * c:CK * (c + 1), :].rearrange("p k h -> p (k h)"),
                                       ACT.Copy).then_inc(s_hi, 1)
                act.nop()

            slots(act, step)

        @block.vector
        def _(dve):
            n_steps = [0]

            def link(ins):
                n_steps[0] += 1
                ins.then_inc(s_v, 1)
                dve.wait_ge(s_v, n_steps[0])

            dve.sem_inc(s_free, 2)
            dve.wait_ge(s_par, 16 * 7)
            dve.reciprocal(dv(INV1), par[:, 0:1])
            dve.reciprocal(dv(INV2), par[:, 2:3])
            dve.tensor_scalar(dv(D1), par[:, 1:2], -1.0, QMID, ALU.mult, ALU.add)
            link(dve.tensor_scalar(dv(D2), par[:, 3:4], -1.0, QMID, ALU.mult, ALU.add))
            dve.wait_ge(s_tanh, 1)
            link(dve.tensor_scalar(dv(C1), dv(TX), par[:, 0:1], par[:, 2:3], ALU.mult, ALU.mult))
            dve.tensor_scalar(dv(C2), dv(TF), 1.0 / TOPK, None, ALU.mult)
            dve.tensor_scalar(dv(C1D1), dv(C1), dv(D1), None, ALU.mult)
            link(dve.tensor_scalar(dv(C1D2), dv(C1), dv(D2), None, ALU.mult))
            dve.tensor_scalar(dv(C1KDD), dv(C1D1), dv(D2), float(D), ALU.mult, ALU.mult).then_inc(s_drv, 1)
            dve.wait_ge(s_drv, 1)
            dve.wait_ge(s_const, 1)

            def stats(which, i, n_ready):
                for h in range(HB):
                    last = dve.bn_stats(st[:, which, h, :], xt[:, i, h * 512:(h + 1) * 512])
                link(last)
                last = dve.bn_aggr(mv[:, which, i, :], st[:, which, :, :].rearrange("p a b -> p (a b)"))
                if n_ready:
                    last.then_inc(s_var[which], 1)
                    dve.wait_ge(s_var[which], n_ready)
                else:
                    link(last)

            def scales(which, i, n, count):
                v = lambda c: lnv[:, which, c, i:i + n]
                mean, var = mv[:, which, i:i + n, 0], mv[:, which, i:i + n, 1]
                dve.wait_ge(s_std[which], count)
                link(dve.reciprocal(v(RST), v(STD)))
                link(dve.scalar_tensor_tensor(v(T1), var, eps[:, :], v(RST), ALU.add, ALU.mult))
                link(dve.scalar_tensor_tensor(v(T2), v(T1), -0.5, v(RST), ALU.mult, ALU.mult))
                if which == 0:
                    link(dve.scalar_tensor_tensor(v(T1), v(T2), 1.5, v(RST), ALU.add, ALU.mult))
                    link(dve.tensor_scalar(v(AA), v(T1), dv(INV1), None, ALU.mult))
                    link(dve.scalar_tensor_tensor(v(T2), mean, -1.0, v(AA), ALU.mult, ALU.mult))
                    last = dve.tensor_scalar(v(BB), v(T2), par[:, 1:2], None, ALU.add)
                else:
                    link(dve.scalar_tensor_tensor(v(AA), v(T2), 1.5, v(RST), ALU.add, ALU.mult))
                    last = dve.scalar_tensor_tensor(v(BB), mean, -1.0, v(AA), ALU.mult, ALU.mult)
                last.then_inc(s_ab[which], 1)
                dve.wait_ge(s_ab[which], count)

            def quantise_x(i):
                link(dve.tensor_scalar(u8x[:, i % 2, :], xt[:, i, :], lnv[:, 0, AA, i:i + 1], lnv[:, 0, BB, i:i + 1],
                                       ALU.mult, ALU.add))
                if i >= 2:
                    dve.wait_ge(s_qt, i - 1)
                dve.tensor_scalar(q1[:, i % 2, :], u8x[:, i % 2, :], 1.0, -QMID, ALU.mult, ALU.add).then_inc(s_q1, 1)

            def x_new(i):
                dve.wait_ge(s_att, i + 2 + i // TPB)
                dve.wait_ge(s_xc, i + 1)
                dve.scalar_tensor_tensor(xt[:, i, :], ps[(i + 1 + i // TPB) % 2][:, :], dv(C1), xt[:, i, :],
                                         ALU.mult, ALU.add).then_inc(s_xn, 1)
                dve.wait_ge(s_xn, i + 1)

            def read_rowsums(b):
                r = slice(b * TPB, (b + 1) * TPB)
                dve.tensor_scalar(rsum[:, r], ps_s[:, RS_C + b * TPB:RS_C + (b + 1) * TPB], dv(C1D2), None,
                                  ALU.mult).then_inc(s_rs, 1)

            def select(b):
                r = slice(b * TPB, (b + 1) * TPB)
                g0 = GT_C + b * TPB * E
                dve.tensor_tensor(lg[:, :, :], ps_s[:, g0:g0 + TPB * E].rearrange("p (i e) -> p i e", e=E),
                                  bg[:, :].unsqueeze(1).to_broadcast([P, TPB, E]), ALU.add).then_inc(s_sread, 1)
                dve.wait_ge(s_sread, 2 * b + 2)
                other = lg[:, :, :].unsqueeze(2).to_broadcast([P, TPB, E, E])
                own = lg[:, :, :].unsqueeze(3).to_broadcast([P, TPB, E, E])
                first = tri[:, 0:E, :].unsqueeze(1).to_broadcast([P, TPB, E, E])
                link(dve.tensor_tensor(pw[:, 1], other, own, ALU.is_equal))
                dve.tensor_tensor(pw[:, 0], other, own, ALU.is_gt)
                link(dve.tensor_tensor(pw[:, 2], pw[:, 1], first, ALU.mult))
                link(dve.tensor_tensor(pw[:, 3], pw[:, 2], pw[:, 0], ALU.add))
                link(dve.tensor_reduce(rank[:, :, :], pw[:, 3], axis=AX.X, op=ALU.add))
                dve.tensor_scalar(sel[:, r, :], rank[:, :, :], float(TOPK), None, ALU.is_lt).then_inc(s_sel, 1)
                dve.wait_ge(s_sel, b + 1)
                link(dve.tensor_scalar(flip[:, :, :], sel[:, r, :], -2.0, 1.0, ALU.mult, ALU.add))
                dve.tensor_tensor(sgn[:, r, :], flip[:, :, :], tok1[:, r].unsqueeze(2).to_broadcast([P, TPB, E]), ALU.mult)
                link(dve.scalar_tensor_tensor(nback[:, :, :], rank[:, :, :], float(TOPK),
                                              back[:, r].unsqueeze(2).to_broadcast([P, TPB, E]), ALU.is_ge, ALU.mult))

            def positions(b):
                r = slice(b * TPB, (b + 1) * TPB)
                c0 = CU_C + b * TPB * E
                link(dve.tensor_tensor(pos[:, :, :], nback[:, :, :],
                                       ps_s[:, c0:c0 + TPB * E].rearrange("p (i e) -> p i e", e=E), ALU.add))
                link(dve.tensor_scalar(pH[:, r, :], pos[:, :, :], 1.0 / P, -0.498, ALU.mult, ALU.add))
                link(dve.scalar_tensor_tensor(pL[:, r, :], pH[:, r, :], -float(P), pos[:, :, :], ALU.mult, ALU.add))

            def make_onehots(b):
                for i in range(b * TPB, (b + 1) * TPB):
                    dve.tensor_tensor(onehot[i][:, :, :], pL[:, i, :].unsqueeze(1).to_broadcast([P, P, E]),
                                      iota_pe[:, :, :], ALU.is_equal).then_inc(s_oh, 1)

            for i in range(0, TPB + 2, 2):
                for j in (i, i + 1):
                    dve.wait_ge(s_x[j], 16)
                    stats(0, j, i // 2 + 1 if j > i else 0)
                scales(0, i, 2, i // 2 + 1)
                quantise_x(i)
                quantise_x(i + 1)
            for i in range(NT):
                x_new(i)
                stats(1, i, i + 1)
                if i == 0:
                    for j in (NT - 2, NT - 1):
                        dve.wait_ge(s_x[j], 16)
                        stats(0, j, NT // 2 if j == NT - 1 else 0)
                if i == TPB - 1:
                    dve.wait_ge(s_small, TPB)
                    read_rowsums(0)
                    dve.wait_ge(s_rs, 1)
                    dve.sem_inc(s_sread, 1)
                scales(1, i, 1, i + 1)
                if i == 0:
                    scales(0, NT - 2, 2, NT // 2)
                    quantise_x(NT - 2)
                if i == 1:
                    quantise_x(NT - 1)
                if i == TPB + 1:
                    dve.wait_ge(s_small, TPB + 2)
                    select(0)
            dve.wait_ge(s_small, NT)
            read_rowsums(1)
            positions(0)
            dve.wait_ge(s_rs, 2)
            dve.sem_inc(s_sread, 1)
            make_onehots(0)
            dve.wait_ge(s_small, NT + 2)
            select(1)
            dve.wait_ge(s_small, NT + 3)
            positions(1)
            make_onehots(1)

            count, base_ = cnt[:, 0, 0:E], cnt[:, 1, :]
            link(dve.tensor_scalar(cnt8[:, :], ps_s[:, CU_C + NT * E:CU_C + (NT + 1) * E], 1.0 / P, 0.494, ALU.mult, ALU.add))
            link(dve.tensor_scalar(count, cnt8[:, :], 1.0, None, ALU.max))
            link(dve.tensor_tensor(tri9[:, :, :], tri[:, :, :], count.unsqueeze(1).to_broadcast([P, E + 1, E]), ALU.mult))
            link(dve.tensor_reduce(base_, tri9[:, :, :], axis=AX.X, op=ALU.add))
            link(dve.tensor_tensor(sid[:, :, :], pH[:, :, :], count.unsqueeze(1).to_broadcast([P, NT, E]), ALU.is_ge))
            link(dve.scalar_tensor_tensor(sid[:, :, :], sid[:, :, :], 1000.0, pH[:, :, :], ALU.mult, ALU.add))
            link(dve.tensor_tensor(sid_h[:, :, :], sid[:, :, :], base_[:, 0:E].unsqueeze(1).to_broadcast([P, NT, E]), ALU.add))
            per_slot = lambda a: a.rearrange("p i e -> p (i e)").unsqueeze(1).to_broadcast([P, NS, NT * E])
            merged = lambda a: a.ap().rearrange("p s i e -> p s (i e)")
            link(dve.tensor_tensor(merged(cmp), per_slot(sid_h[:, :, :]), merged(iota_se), ALU.is_equal))
            dve.tensor_tensor(merged(R), merged(cmp), per_slot(sgn[:, :, :]), ALU.mult).then_inc(s_R, 1)
            slot_no = iota_f[:, 0:NS].unsqueeze(2).to_broadcast([P, NS, E - 1])
            ends = base_[:, 1:E].unsqueeze(1).to_broadcast([P, NS, E - 1])
            starts = base_[:, 0:E - 1].unsqueeze(1).to_broadcast([P, NS, E - 1])
            s7 = sc26[:, :, 0:E - 1]
            link(dve.tensor_tensor(s7, slot_no, ends, ALU.is_ge))
            link(dve.tensor_reduce(sv[:, 0, :], s7, axis=AX.X, op=ALU.add))
            link(dve.tensor_tensor(s7, slot_no, starts, ALU.is_equal))
            link(dve.tensor_tensor(s7, s7, iota_f[:, 1:E].unsqueeze(1).to_broadcast([P, NS, E - 1]), ALU.mult))
            link(dve.tensor_reduce(sv[:, 1, :], s7, axis=AX.X, op=ALU.add))
            link(dve.tensor_scalar(svi[:, :], sv[:, 0, :], 0.5, -0.25, ALU.mult, ALU.add))
            link(dve.tensor_copy(sv[:, 2, :], svi[:, :]))
            link(dve.scalar_tensor_tensor(sv[:, 3, :], sv[:, 2, :], -2.0, sv[:, 0, :], ALU.mult, ALU.add))
            dve.tensor_scalar(tab[:, NEED:NEED + NS], sv[:, 0, :], 1.0, None, ALU.add)
            dve.tensor_scalar(tab[:, WOFF:WOFF + NS], sv[:, 3, :], float(WSZ), None, ALU.mult)
            dve.tensor_copy(tab[:, NXT:NXT + NS], sv[:, 1, :])
            dve.tensor_copy(tab[:, BAS:BAS + E + 1], base_).then_inc(s_tab, 1)
            dve.wait_ge(s_idx_ps, 1)
            link(dve.tensor_copy(sv[:, 4, :], ps_s[:, 0:NS]))
            link(dve.scalar_tensor_tensor(sv[:, 5, :], sv[:, 4, :], -1.0, sv[:, 4, :], ALU.mult, ALU.max))
            dve.tensor_scalar(idx[:, :], sv[:, 5, :], 1.0, -1.0, ALU.max, ALU.add)
            dve.tensor_scalar(weight[:, :], ps_s[:, 0:NS], 0.0, dv(C2), ALU.is_lt, ALU.mult).then_inc(s_idx, 1)
            dve.wait_ge(s_idx, 1)
            dve.wait_ge(s_tab, 1)

            def evacuate_lo(q):
                dve.tensor_tensor(yT_lo[q][:, :, :], ps_y[:, :, :], yT_hi[q][:, :, :].bitcast(f32),
                                  ALU.subtract).then_inc(s_el, 1)

            def split_lo(c, chunk_no, dst):
                dve.wait_ge(s_hi, chunk_no)
                dve.tensor_tensor(w_lo[:, dst], stage[:, CK * c:CK * (c + 1), :].rearrange("p k h -> p (k h)"),
                                  w_hi[:, dst].bitcast(f32), ALU.subtract).then_inc(s_lo, 1)

            for c in range(NLO):
                split_lo(c, c + 1, slice(c * CW, (c + 1) * CW))
            dve.wait_ge(s_eh, 1)
            evacuate_lo(0)
            dve.wait_ge(s_oi, 16 * NT)

            def step(slot, q, turn):
                dve.wait_ge(s_eh, slot + 2)
                evacuate_lo(1 - q)
                nxt = entry(dve, NXT, slot, E - 1)
                with dve.If(nxt > 0):
                    dst = dve.snap((nxt & 1) * WSZ)
                    for c in range(NLO):
                        split_lo(c, nxt * NCH + c + 1, bass.ds(dst + c * CW, CW))
                woff = entry(dve, WOFF, slot, WSZ)
                expert1 = entry(dve, NEED, slot, E)
                for b in range(2):
                    with dve.If(woff == b * WSZ):
                        dve.wait_ge(s_bias[b], ((expert1 + 1) >> 1) * 16)
                        settle(dve)
                dve.wait_ge(s_mm, slot + 2)
                dve.wait_ge(s_resf, slot + 1)
                dve.tensor_tensor(res[q][:, :], ps[q][:, :], bias[:, bass.ds(woff >> 3, D)], ALU.add).then_inc(s_free, 1)
                dve.wait_ge(s_free, slot + 3)
                dve.tensor_scalar(res[q][:, :], res[q][:, :], 0.0, weight[:, bass.ds(slot, 1)],
                                  ALU.max, ALU.mult).then_inc(s_post, 1)

            slots(dve, step)

        @block.tensor
        def _(pe):
            pe.wait_ge(s_const, 1)

            def transpose_q1(i):
                pe.wait_ge(s_q1, i + 1)
                if i >= 1:
                    pe.wait_ge(s_qe, i)
                for k in range(KT):
                    last = pe.transpose(ps_q[:, k, :], q1[:, i % 2, k * P:(k + 1) * P], ident_b[:, :])
                last.then_inc(s_qt, 1)

            def column_sums(b):
                u = b * (TPB + 1)
                if u >= 2:
                    pe.wait_ge(s_xn, u - 2)
                for k in range(KT):
                    pe.wait_ge(s_q2, b * KT + k + 1)
                    for h in range(HB):
                        last = pe.matmul(ps[u % 2][:, h * 512:(h + 1) * 512], ones_b[:, :],
                                         q2[:, b * KT + k, h * 512:(h + 1) * 512], start=(k == 0), stop=(k == KT - 1))
                last.then_inc(s_att, 1)

            def attention(i):
                b = i // TPB
                u = i + 1 + b
                if u == 2 or u == TPB + 3:
                    pe.wait_ge(s_corr, b + 1)
                if i >= 2 and u != TPB + 3:
                    pe.wait_ge(s_xn, i - 1 if i != TPB else TPB)
                for k in range(KT):
                    for h in range(HB):
                        last = pe.matmul(ps[u % 2][:, h * 512:(h + 1) * 512], q1T[:, i, k, :],
                                         q2[:, b * KT + k, h * 512:(h + 1) * 512], start=(k == 0), stop=(k == KT - 1))
                last.then_inc(s_att, 1)

            def transpose_y(i):
                pe.wait_ge(s_y, i + 1)
                if i >= 1:
                    pe.wait_ge(s_ye, i)
                for k in range(KT):
                    last = pe.transpose(ps_y[:, k, :], y[i % 2][:, k * P:(k + 1) * P], ident_f[:, :])
                last.then_inc(s_yt, 1)

            def small(i):
                for group, reads in ((TPB, 1), (TPB + 2, 2), (NT, 3), (NT + 2, 4)):
                    if i == group:
                        pe.wait_ge(s_sread, reads)
                if i < NT:
                    for k in range(KT):
                        last = pe.matmul(ps_s[:, RS_C + i:RS_C + i + 1], q1T[:, i, k, :], ones_b[:, 0:1],
                                         start=(k == 0), stop=(k == KT - 1))
                if 2 <= i < NT + 2:
                    pe.wait_ge(s_ye, i - 1)
                    g = GT_C + (i - 2) * E
                    for k in range(KT):
                        last = pe.matmul(ps_s[:, g:g + E], yT[i % 2][:, k, :], wg[:, k, :],
                                         start=(k == 0), stop=(k == KT - 1))
                if i in (NT - 1, NT + 2):
                    b = 0 if i < NT else 1
                    first, end = b * TPB, TPB if b == 0 else NT + 1
                    pe.wait_ge(s_sel, b + 1)
                    cols = lambda a: ps_s[:, CU_C + a * E:CU_C + end * E].rearrange("p (i e) -> p i e", e=E)
                    pe.matmul(cols(first), before[:, :], sel[:, first:end, :], start=True, stop=False)
                    for j in range(min(end - 1, NT)):
                        a = max(first, j + 1)
                        last = pe.matmul(cols(a), ones_b[:, :], sel[:, j:j + 1, :].to_broadcast([P, end - a, E]),
                                         start=False, stop=(j == min(end - 1, NT) - 1))
                last.then_inc(s_small, 1)

            for i in range(TPB):
                transpose_q1(i)
            column_sums(0)
            for i in range(NT + 3):
                if i == TPB:
                    column_sums(1)
                if i < NT:
                    attention(i)
                if i == 2:
                    pe.wait_ge(s_wg, 16)
                small(i)
                if 1 <= i <= NT:
                    transpose_y(i - 1)
                if i <= 1:
                    transpose_q1(TPB + 2 * i)
                    transpose_q1(TPB + 2 * i + 1)
            pe.wait_ge(s_R, 1)
            for i in range(NT):
                pe.wait_ge(s_oh, i + 1)
                for e in range(E):
                    last = pe.matmul(ps_s[:, 0:NS], onehot[i][:, :, e], R[:, :, i, e],
                                     start=(i == 0 and e == 0), stop=(i == NT - 1 and e == E - 1))
            last.then_inc(s_idx_ps, 1)

            def transpose_slot(q):
                for k in range(KT):
                    last = pe.transpose(ps_y[:, k, :], y_rows[q][:, k * P:(k + 1) * P], ident_f[:, :])
                last.then_inc(s_tp, 1)

            pe.wait_ge(s_tab, 1)
            pe.wait_ge(s_idx_ps, 1)
            pe.sem_inc(s_mm, 1)
            pe.wait_ge(s_g[0], 16)
            transpose_slot(0)

            def step(slot, q, turn):
                pe.wait_ge(s_g[1 - q], turn * 16 + (16 if q == 0 else 32))
                pe.wait_ge(s_el, slot + 1)
                transpose_slot(1 - q)
                expert1 = entry(pe, NEED, slot, E)
                pe.wait_ge(s_lo, expert1 * NLO)
                pe.wait_ge(s_lop, expert1)
                woff = entry(pe, WOFF, slot, WSZ)
                pe.wait_ge(s_free, slot + 1)
                for k in range(KT):
                    for lhs, w in ((yT_hi, w_hi), (yT_hi, w_lo), (yT_lo, w_hi)):
                        for h in range(HB):
                            last = pe.matmul(ps[q][:, h * 512:(h + 1) * 512], lhs[q][:, k, :],
                                             w[:, bass.ds(woff + k * D + h * 512, 512)],
                                             start=(k == 0 and lhs is yT_hi and w is w_hi),
                                             stop=(k == KT - 1 and lhs is yT_lo))
                last.then_inc(s_mm, 1)

            slots(pe, step)


_INS = ["x", "ctx_4096", "g_xattn", "g_ffn", "L0_xattn_x1_scale", "L0_xattn_x1_zp", "L0_xattn_x2_scale",
        "L0_xattn_x2_zp", "L0_ffn_W_gate", "L0_ffn_b_gate", "L0_ffn_W_e", "L0_ffn_b_e"]
_OUTS = [((2, 512, 1024), "float32")]


def kernel(**inputs):
    import numpy as _np
    import concourse.bacc as _bacc
    from concourse import mybir as _mybir
    from concourse.bass_utils import run_bass_kernel_spmd as _run

    nc = _bacc.Bacc("TRN2", target_bir_lowering=False, num_devices=1)
    arrays, args = {}, []
    for name in _INS:
        a = _np.ascontiguousarray(inputs[name])
        arrays[f"in_{name}_dram"] = a
        args.append(nc.dram_tensor(f"in_{name}_dram", a.shape, _mybir.dt.from_np(a.dtype), kind="ExternalInput").ap())
    for i, (shape, dtype) in enumerate(_OUTS):
        dt = _mybir.dt.from_np(_np.dtype(dtype))
        args.append(nc.dram_tensor(f"out_{i}_dram", shape, dt, kind="ExternalOutput").ap())
    flamingo_gated_moe(nc, *args)
    r = _run(nc, [arrays], core_ids=[0])
    got = tuple(r.results[0][f"out_{i}_dram"] for i in range(len(_OUTS)))
    return got[0]
```

```python
import concourse.bass as bass
from concourse import mybir
from contextlib import ExitStack


def flamingo_gated_moe(nc, x, ctx_kv, g_xattn, g_ffn, x1_scale, x1_zp, x2_scale, x2_zp,
                       W_gate, b_gate, W_e, b_e, out):
    f32, f32r, bf16, f16 = mybir.dt.float32, mybir.dt.float32r, mybir.dt.bfloat16, mybir.dt.float16
    i32, u32, u8 = mybir.dt.int32, mybir.dt.uint32, mybir.dt.uint8
    ALU, ACT = mybir.AluOpType, mybir.ActivationFunctionType
    AX = mybir.AxisListType

    P = 128
    B, S, D = x.shape
    E = W_e.shape[0]
    KT = D // P
    NT = B * S // P
    TPB = S // P
    HB = D // 512
    TOPK = 2
    MAX_SLOTS = (TOPK * NT * P - E) // P + E
    SPE = B * S // P
    NS = MAX_SLOTS + 4
    QMID = 128.0
    EPS = 1e-5
    WSZ = KT * D
    NCH = 4
    CK = KT // NCH
    CW = WSZ // NCH
    NLO = NCH - 1

    x_t = x.rearrange("b (n p) d -> (b n) p d", p=P)
    out_rows = out.rearrange("b s d -> (b s) d")
    out_t = out.rearrange("b (n p) d -> (b n) p d", p=P)
    ctx_t = ctx_kv.rearrange("b (k p) d -> (b k) p d", p=P)
    w_t = W_e.rearrange("e (k p) h -> p e k h", p=P)
    y_dram = nc.dram_tensor("y_scratch", (NT * P, D), f32, kind="Internal").ap()
    y_t = y_dram.rearrange("(n p) d -> n p d", p=P)

    ctx = ExitStack()
    with ctx:
        def sb(name, shape, dt):
            return ctx.enter_context(nc.sbuf_tensor(name, shape, dt))

        def sem(name):
            return ctx.enter_context(nc.semaphore(name))

        KB = 1024
        arena = sb("arena", [P, 200 * KB], u8)
        base = nc.sbuf_base - 200 * KB

        def at(name, shape, dt, off):
            return nc.alloc_sbuf_tensor_at(name, shape, dt, offset=base + off)

        WHI, WLO, STG, YT, GB, RES, BIA = 0, 64 * KB, 128 * KB, 160 * KB, 176 * KB, 184 * KB, 192 * KB
        w_hi = at("w_hi", [P, 2 * WSZ], f32r, WHI)
        w_lo = at("w_lo", [P, 2 * WSZ], f32r, WLO)
        stage = at("stage", [P, KT, D], f32, STG)
        yT_hi = [at(f"yT_hi{q}", [P, KT, P], f32r, YT + 4 * KB * q) for q in range(2)]
        yT_lo = [at(f"yT_lo{q}", [P, KT, P], f32r, YT + 8 * KB + 4 * KB * q) for q in range(2)]
        y_rows = [at(f"y_rows{q}", [P, D], f32, GB + 4 * KB * q) for q in range(2)]
        res = [at(f"res{q}", [P, D], f32, RES + 4 * KB * q) for q in range(2)]
        bias = at("bias", [P, 2 * D], f32, BIA)
        xt = at("xt", [P, NT, D], f32, WHI + 32 * KB)
        q1T = at("q1T", [P, NT, KT, P], bf16, WLO + 16 * KB)
        q2 = at("q2", [P, B * KT, D], bf16, WLO + 32 * KB)
        q1 = at("q1", [P, 2, D], bf16, RES)
        yT = [at(f"yT{q}", [P, KT, P], f32, YT + 4 * KB * q) for q in range(2)]
        y = [at(f"y{q}", [P, D], f32, GB + 4 * KB * q) for q in range(2)]
        CB = 6
        corr = stage[:, CB:CB + B, :]
        u8x = sb("u8x", [P, 2, D], u8)
        u8c = at("u8c", [P, 2, D], u8, RES + 4 * KB)

        ident_b = sb("ident_b", [P, P], bf16)
        ident_f = sb("ident_f", [P, P], f32)
        ones_b = at("ones_b", [P, P], bf16, YT + 8 * KB)
        before = at("before", [P, P], bf16, YT + 8 * KB + 256)
        iota_f = at("iota_f", [P, 32], f32, YT + 8 * KB + 512)
        wg = at("wg", [P, KT, E], f32, YT + 10 * KB)
        tri = at("tri", [P, E + 1, E], f32, YT + 10 * KB + 256)
        iota_pe = at("iota_pe", [P, P, E], bf16, WLO + 32 * KB)
        pw = at("pw", [P, 4, TPB, E, E], bf16, WLO + 34 * KB)
        cmp = at("cmp", [P, NT * E, SPE], f16, WLO + 36 * KB)
        R = at("R", [P, NT * E, SPE], f16, WLO + 37 * KB)
        onehot = [at(f"onehot{i}", [P, P, E], bf16, WLO + 48 * KB + 2 * KB * i) for i in range(NT)]
        tok1 = sb("tok1", [P, NT], f32)
        back = sb("back", [P, NT], f32)
        par = sb("par", [P, 6], f32)
        bg = sb("bg", [P, E], f32)
        drv = sb("drv", [P, 16], f32)
        INV1, INV2, D1, D2, C1, C1D1, C1D2, C1KDD, C2, TX, TF, TMP = range(12)

        def dv(c):
            return drv[:, c:c + 1]

        eps = sb("eps", [P, 1], f32)
        st = sb("st", [P, 2, HB, 6], f32)
        mv = sb("mv", [P, 2, NT, 2], f32)
        lnv = sb("lnv", [P, 2, 6, NT], f32)
        STD, RST, T1, T2, AA, BB = range(6)
        rsum = sb("rsum", [P, NT], f32)
        lg = sb("lg", [P, TPB, E], f32)
        rank = sb("rank", [P, TPB, E], f32)
        sel = sb("sel", [P, NT + 1, E], bf16)
        flip = sb("flip", [P, TPB, E], f32)
        sgn = sb("sgn", [P, NT, E], f16)
        nback = sb("nback", [P, TPB, E], f32)
        pos = sb("pos", [P, TPB, E], f32)
        pH = sb("pH", [P, NT, E], u8)
        pL = sb("pL", [P, NT, E], bf16)
        cnt = sb("cnt", [P, 6, 9], f32)
        cnt8 = sb("cnt8", [P, E], u8)
        tri9 = sb("tri9", [P, E + 1, E], f32)
        sc = at("sc", [P, 2, NS, E - 1], f32, RES + 6 * KB)
        sv = at("sv", [P, 6, NS], f32, RES + 5 * KB)
        tokens = sb("tokens", [P, 2, E * SPE], f32)
        svi = sb("svi", [P, NS], u8)
        tab = sb("tab", [P, 4 * NS + E + 1], i32)
        EXPERT, WOFF, NXT, COL, BAS = 0, NS, 2 * NS, 3 * NS, 4 * NS
        idx = sb("idx", [P, (E + 1) * SPE], u32)
        weight = sb("weight", [P, E * SPE], f32)
        gidx = sb("gidx", [P, 2], u32)
        sidx = sb("sidx", [P, 2], u32)

        ps = [ctx.enter_context(nc.psum_tensor(f"ps{i}", [P, HB * 512], f32)) for i in range(2)]
        ps_q = ctx.enter_context(nc.psum_tensor("ps_q", [P, KT, P], bf16))
        ps_y = ctx.enter_context(nc.psum_tensor("ps_y", [P, KT, P], f32))
        ps_s = ctx.enter_context(nc.psum_tensor("ps_s", [P, 512], f32))
        RS_C, GT_C, CU_C = 0, NT, NT + NT * E

        s_par = sem("scales_landed")
        s_gpar = sem("gates_landed")
        s_wg = sem("gate_landed")
        s_x = [sem(f"x_landed{i}") for i in range(NT)]
        s_ctx = [sem(f"ctx_landed{i}") for i in range(CB)]
        s_w = [sem(f"w_landed{c}") for c in range(NCH)]
        s_bias = [sem(f"bias_landed{q}") for q in range(2)]
        s_const = sem("consts_made")
        s_cstep = sem("const_step")
        s_inv = sem("inverse_scales_ready")
        s_tanh = sem("tanh_done")
        s_drv = sem("params_derived")
        s_v = sem("dve_step")
        s_var = [sem("var1_ready"), sem("var2_ready")]
        s_std = [sem("std1_ready"), sem("std2_ready")]
        s_ab = [sem("scale1_ready"), sem("scale2_ready")]
        s_xq = sem("x_quantised")
        s_q1 = sem("q1_ready")
        s_qt = sem("q1T_in_psum")
        s_qe = sem("q1T_ready")
        s_uc = sem("ctx_quantised")
        s_q2 = sem("q2_ready")
        s_att = sem("attn_in_psum")
        s_small = sem("small_in_psum")
        s_sread = sem("small_read")
        s_corr = sem("corr_ready")
        s_xc = sem("x_plus_corr")
        s_xn = sem("x_new_ready")
        s_y = sem("y_ready")
        s_oa = sem("x_new_with_rowsum")
        s_rs = sem("rowsums_ready")
        s_oi = sem("x_new_stored")
        s_ys = [sem(f"y_stored{q}") for q in range(2)]
        s_yt = sem("yT_in_psum")
        s_ye = sem("yT_ready")
        s_sel = sem("selection_ready")
        s_cnt = sem("counts_in_psum")
        s_iota = sem("positions_pattern_ready")
        s_oh = sem("onehots_ready")
        s_R = sem("slot_matrix_ready")
        s_idx_ps = sem("indices_in_psum")
        s_idx = sem("indices_ready")
        s_col = sem("columns_ready")
        s_tab = sem("schedule_ready")
        s_hi = sem("w_hi_done")
        s_lo = sem("w_lo_done")
        s_lop = sem("w_lo_last_done")
        s_pool = sem("pool_step")
        s_g = [sem(f"gathered{q}") for q in range(2)]
        s_tp = sem("slot_yT_in_psum")
        s_eh = sem("slot_yT_hi_ready")
        s_el = sem("slot_yT_lo_ready")
        s_mm = sem("slot_matmuls_done")
        s_free = sem("slot_psum_free")
        s_post = sem("slot_result_ready")
        s_resf = sem("slot_result_free")
        s_sc = sem("slot_scattered")
        s_settled = sem("waits_settled")

        block = ctx.enter_context(nc.Block())

        def slots(eng, body):
            n_used = eng.value_load(tab[0:1, BAS + E:BAS + E + 1], min_val=E, max_val=MAX_SLOTS)
            with eng.Fori(0, (MAX_SLOTS + 1) // 2) as turn:
                for q in range(2):
                    with eng.If(turn * 2 + q < n_used):
                        body(turn * 2 + q, q, turn)
            return n_used

        def entry(eng, field, slot, hi, lo=0):
            return eng.value_load(tab[0:1, bass.ds(slot + field, 1)], min_val=lo, max_val=hi)

        def settle(eng):
            eng.sem_inc(s_settled, 1)

        @block.sync
        def _(sp):
            def load_ctx(k):
                if k >= CB:
                    sp.wait_ge(s_uc, k - CB + 1)
                sp.dma_start(stage[:, k % CB, :], ctx_t[k]).then_inc(s_ctx[k % CB], 16)

            def load_x(i):
                sp.dma_start(xt[:, i, :], x_t[i]).then_inc(s_x[i], 16)

            for c, src in enumerate((x1_scale, x1_zp)):
                sp.dma_start(par[:, c:c + 1], src.partition_broadcast(P)).then_inc(s_par, 16)
            for i in range(TPB):
                load_x(i)
                load_ctx(i)
            for k in range(TPB, KT):
                load_ctx(k)
            for i in range(TPB, NT):
                load_x(i)
            sp.dma_start(wg[:, :, :], W_gate.rearrange("(k p) e -> p k e", p=P)).then_inc(s_wg, 16)
            for k in range(KT, 2 * KT):
                load_ctx(k)

            def store_x_new(i):
                sp.wait_ge(s_oa, i + 1)
                sp.dma_start(out_t[i], xt[:, i, :]).then_inc(s_oi, 16)

            sp.wait_ge(s_uc, B * KT)
            for c in range(NLO):
                sp.dma_start(stage[:, CK * c:CK * (c + 1), :], w_t[:, 0, CK * c:CK * (c + 1), :]).then_inc(s_w[c], 16)
            for e in range(2):
                sp.dma_start(bias[:, e * D:(e + 1) * D], b_e[e].partition_broadcast(P)).then_inc(s_bias[e], 16)
            for i in range(TPB):
                store_x_new(i)
            sp.wait_ge(s_xc, NT)
            sp.dma_start(stage[:, CK * NLO:, :], w_t[:, 0, CK * NLO:, :]).then_inc(s_w[NLO], 16)
            for i in range(TPB, NT):
                store_x_new(i)
            with sp.Fori(1, E) as n:
                for c in range(NCH):
                    sp.wait_ge(s_hi, n * NCH - NCH + c + 1)
                    settle(sp)
                    if c < NLO:
                        sp.wait_ge(s_lo, n * NLO - NLO + c + 1)
                    else:
                        sp.wait_ge(s_lop, n)
                    sp.dma_start(stage[:, CK * c:CK * (c + 1), :],
                                 w_t[:, bass.ds(n, 1), CK * c:CK * (c + 1), :].rearrange("p e k h -> p (e k) h")
                                 ).then_inc(s_w[c], 16)
                with sp.If(n > 1):
                    sp.wait_ge(s_post, entry(sp, BAS - 1, n, MAX_SLOTS, lo=1))
                    settle(sp)
                    for q in range(2):
                        with sp.If((n & 1) == q):
                            sp.dma_start(bias[:, q * D:(q + 1) * D],
                                         b_e[bass.ds(n, 1), :].rearrange("a d -> (a d)").partition_broadcast(P)
                                         ).then_inc(s_bias[q], 16)
                    sp.nop()
                sp.nop()

        @block.gpsimd
        def _(pool):
            pool.memset(ident_b[:, :], 0.0)
            pool.memset(ident_f[:, :], 0.0)
            pool.memset(ones_b[:, :], 1.0)
            pool.memset(before[:, :], 1.0)
            pool.memset(tri[:, :, :], 1.0)
            pool.memset(eps[:, :], EPS)
            pool.memset(sel[:, NT, :], 0.0)
            pool.memset(idx[:, E * SPE:], 0)
            pool.iota(iota_f[:, :], [[1, 32]], base=0, channel_multiplier=0, allow_small_or_imprecise_dtypes=True)
            pool.iota(tok1[:, :], [[P, NT]], base=1, channel_multiplier=1, allow_small_or_imprecise_dtypes=True)
            pool.iota(back[:, :], [[-P, NT]], base=NT * P - 1, channel_multiplier=-1,
                      allow_small_or_imprecise_dtypes=True).then_inc(s_cstep, 1)
            pool.wait_ge(s_cstep, 1)
            pool.affine_select(out=ident_b[:, :], in_=ident_b[:, :], compare_op=ALU.not_equal, fill=1.0,
                               base=0, pattern=[[-1, P]], channel_multiplier=1)
            pool.affine_select(out=ident_f[:, :], in_=ident_f[:, :], compare_op=ALU.not_equal, fill=1.0,
                               base=0, pattern=[[-1, P]], channel_multiplier=1)
            pool.affine_select(out=before[:, :], in_=before[:, :], compare_op=ALU.is_gt, fill=0.0,
                               base=0, pattern=[[1, P]], channel_multiplier=-1)
            pool.affine_select(out=tri[:, :, :], in_=tri[:, :, :], compare_op=ALU.is_gt, fill=0.0,
                               base=0, pattern=[[1, E + 1], [-1, E]], channel_multiplier=0).then_inc(s_const, 1)
            pool.sem_inc(s_resf, 2)

            def centre_ctx(k):
                pool.wait_ge(s_uc, k + 1)
                pool.tensor_scalar(q2[:, k, :], u8c[:, k % 2, :], 1.0, -QMID, ALU.mult, ALU.add).then_inc(s_q2, 1)

            def add_corr(i):
                pool.wait_ge(s_corr, i // TPB + 1)
                if i in (0, TPB):
                    pool.wait_ge(s_q1, i + TPB)
                pool.tensor_tensor(xt[:, i, :], xt[:, i, :], corr[:, i // TPB, :], ALU.add).then_inc(s_xc, 1)

            def add_rowsum(i):
                pool.wait_ge(s_y, i + 1)
                pool.tensor_scalar(xt[:, i, :], xt[:, i, :], 1.0, rsum[:, i:i + 1], ALU.mult, ALU.add).then_inc(s_oa, 1)

            def centre_q1(i):
                pool.wait_ge(s_xq, i - TPB + 1)
                pool.wait_ge(s_qt, i - 1)
                pool.tensor_scalar(q1[:, i % 2, :], u8x[:, i % 2, :], 1.0, -QMID, ALU.mult, ALU.add).then_inc(s_q1, 1)

            def split_lo0(c):
                pool.wait_ge(s_hi, c + 1)
                if c == NCH // 2:
                    pool.wait_ge(s_att, NT + B)
                pool.tensor_tensor(w_lo[:, c * CW:(c + 1) * CW], stage[:, CK * c:CK * (c + 1), :].rearrange("p k h -> p (k h)"),
                                   w_hi[:, c * CW:(c + 1) * CW].bitcast(f32), ALU.subtract
                                   ).then_inc(s_lo if c < NLO else s_lop, 1)

            for k in range(KT):
                centre_ctx(k)
            add_corr(0)
            centre_q1(TPB)
            centre_q1(TPB + 1)
            add_corr(1)
            centre_ctx(KT)
            centre_q1(TPB + 2)
            centre_q1(TPB + 3)
            add_corr(2)
            for k in range(KT + 1, KT + 4):
                centre_ctx(k)
            add_corr(3)
            for k in range(KT + 4, 2 * KT):
                centre_ctx(k)
            pool.wait_ge(s_att, TPB + 1)
            pool.iota(iota_pe[:, :, :], [[1, P], [0, E]], base=0, channel_multiplier=0,
                      allow_small_or_imprecise_dtypes=True).then_inc(s_iota, 1)
            add_corr(TPB)
            pool.wait_ge(s_rs, 1)
            for i in range(TPB):
                add_rowsum(i)
                if i < TPB - 1:
                    add_corr(TPB + 1 + i)
            for c in range(NCH // 2):
                split_lo0(c)
            for i in range(TPB, NT):
                add_rowsum(i)
            for c in range(NCH // 2, NCH):
                split_lo0(c)

            def gather(slot, q, step):
                col = entry(pool, COL, slot, (E + 1) * SPE - 1)
                pool.tensor_copy(gidx[:, q:q + 1], idx[:, bass.ds(col, 1)]).then_inc(s_pool, 1)
                pool.wait_ge(s_pool, step)
                settle(pool)
                pool.indirect_dma_start(out=y_rows[q][:, :], out_offset=None, in_=y_dram[:, :],
                                        in_offset=bass.IndirectOffsetOnAxis(ap=gidx[:, q:q + 1], axis=0)
                                        ).then_inc(s_g[q], 16)

            pool.wait_ge(s_idx, 1)
            pool.wait_ge(s_col, 1)
            for q in range(2):
                pool.wait_ge(s_ys[q], 16 * NT // 2)
            pool.wait_ge(s_oi, 16 * NT)
            for q in range(2):
                gather(q, q, q + 1)

            def split_lo_last(chunk_no, dst):
                pool.wait_ge(s_hi, chunk_no)
                pool.tensor_tensor(w_lo[:, dst], stage[:, CK * NLO:, :].rearrange("p k h -> p (k h)"),
                                   w_hi[:, dst].bitcast(f32), ALU.subtract).then_inc(s_lop, 1)

            pool.wait_ge(s_tp, 1)
            gather(2, 0, 3)

            def step(slot, q, turn):
                pool.wait_ge(s_tp, slot + 2)
                gather(slot + 3, 1 - q, slot * 2 + 4)
                nxt = entry(pool, NXT, slot, E - 1)
                with pool.If(nxt > 0):
                    split_lo_last(nxt * NCH + NCH, bass.ds((nxt & 1) * WSZ + NLO * CW, CW))
                col = entry(pool, COL, slot, E * SPE - 1)
                pool.tensor_copy(sidx[:, q:q + 1], idx[:, bass.ds(col, 1)]).then_inc(s_pool, 1)
                pool.wait_ge(s_pool, slot * 2 + 5)
                pool.wait_ge(s_post, slot + 1)
                settle(pool)
                pool.indirect_dma_start(out=out_rows[:, :],
                                        out_offset=bass.IndirectOffsetOnAxis(ap=sidx[:, q:q + 1], axis=0),
                                        in_=res[q][:, :], in_offset=None, compute_op=ALU.add).then_inc(s_sc, 16)
                pool.wait_ge(s_sc, slot * 16 + 16)
                pool.sem_inc(s_resf, 1)

            pool.wait_ge(s_tab, 1)
            n = slots(pool, step)
            pool.wait_ge(s_sc, n * 16)
            pool.wait_ge(s_g[0], ((n + 4) >> 1) * 16)
            pool.wait_ge(s_g[1], ((n + 3) >> 1) * 16)

        @block.scalar
        def _(act):
            for c, src in enumerate((x2_scale, x2_zp, g_xattn, g_ffn)):
                act.dma_start(par[:, c + 2:c + 3], src.partition_broadcast(P)).then_inc(s_par if c < 2 else s_gpar, 16)
            act.dma_start(bg[:, :], b_gate.partition_broadcast(P)).then_inc(s_gpar, 16)

            def quantise_ctx(k):
                act.wait_ge(s_ctx[k % CB], 16 * (k // CB + 1))
                if k >= 2:
                    act.wait_ge(s_q2, k - 1)
                act.activation(u8c[:, k % 2, :], stage[:, k % CB, :], ACT.Identity, scale=dv(INV2),
                               bias=par[:, 3:4]).then_inc(s_uc, 1)

            def std(which, i, n, count):
                act.wait_ge(s_var[which], count)
                act.activation(lnv[:, which, STD, i:i + n], mv[:, which, i:i + n, 1], ACT.Sqrt,
                               bias=eps[:, :]).then_inc(s_std[which], 1)

            def keep_q1T(i):
                act.wait_ge(s_qt, i + 1)
                act.activation(q1T[:, i, :, :], ps_q[:, :, :], ACT.Copy).then_inc(s_qe, 1)

            def make_corr(b):
                act.wait_ge(s_att, b * (TPB + 1) + 1)
                act.activation(corr[:, b, :], ps[(b * (TPB + 1)) % 2][:, :], ACT.Identity, scale=dv(C1D1),
                               bias=dv(C1KDD)).then_inc(s_corr, 1)

            def normalise(i):
                act.wait_ge(s_ab[1], i + 1)
                if i >= 2:
                    act.wait_ge(s_ys[i % 2], 16 * (i // 2))
                    act.wait_ge(s_yt, i - 1)
                act.activation(y[i % 2][:, :], xt[:, i, :], ACT.Identity, scale=lnv[:, 1, AA, i:i + 1],
                               bias=lnv[:, 1, BB, i:i + 1]).then_inc(s_y, 1)
                act.wait_ge(s_y, i + 1)
                act.dma_start(y_t[i], y[i % 2][:, :]).then_inc(s_ys[i % 2], 16)

            def keep_yT(i):
                act.wait_ge(s_yt, i + 1)
                if i >= 2:
                    act.wait_ge(s_small, i + 1)
                act.activation(yT[i % 2][:, :, :], ps_y[:, :, :], ACT.Copy).then_inc(s_ye, 1)

            def split_hi0(c):
                act.wait_ge(s_w[c], 16)
                act.activation(w_hi[:, c * CW:(c + 1) * CW], stage[:, CK * c:CK * (c + 1), :].rearrange("p k h -> p (k h)"),
                               ACT.Copy).then_inc(s_hi, 1)

            def quantise_x(i):
                act.wait_ge(s_ab[0], i // 2 + 1)
                if i < TPB + 2:
                    act.wait_ge(s_q1, TPB)
                else:
                    act.wait_ge(s_q1, i - 1)
                act.activation(u8x[:, i % 2, :], xt[:, i, :], ACT.Identity, scale=lnv[:, 0, AA, i:i + 1],
                               bias=lnv[:, 0, BB, i:i + 1]).then_inc(s_xq, 1)

            act.wait_ge(s_inv, 1)
            quantise_ctx(0)
            act.wait_ge(s_gpar, 16 * 3)
            act.activation(drv[:, TX:TF + 1], par[:, 4:6], ACT.Tanh).then_inc(s_tanh, 1)
            quantise_ctx(1)
            std(0, 0, 2, 1)
            quantise_ctx(2)
            quantise_ctx(3)
            keep_q1T(0)
            quantise_ctx(4)
            keep_q1T(1)
            std(0, 2, 2, 2)
            quantise_ctx(5)
            quantise_ctx(6)
            keep_q1T(2)
            quantise_ctx(7)
            keep_q1T(3)
            std(0, 4, 2, 3)
            act.wait_ge(s_drv, 1)
            make_corr(0)
            quantise_x(TPB)
            quantise_x(TPB + 1)
            std(0, 6, 2, 4)
            quantise_ctx(KT)
            keep_q1T(TPB)
            quantise_x(TPB + 2)
            more_ctx = {0: (KT + 1, KT + 2), 1: (KT + 3, KT + 4), 2: (KT + 5, KT + 6), 3: (KT + 7,)}
            for i in range(NT + 1):
                if i == TPB:
                    make_corr(1)
                if i < NT:
                    std(1, i, 1, i + 1)
                if i == 0:
                    keep_q1T(TPB + 1)
                if 1 <= i:
                    keep_yT(i - 1)
                if i < NT:
                    normalise(i)
                if i == 0:
                    quantise_x(TPB + 3)
                if i == 1:
                    keep_q1T(TPB + 2)
                    keep_q1T(TPB + 3)
                for k in more_ctx.get(i, ()):
                    quantise_ctx(k)
                if TPB < i <= TPB + NCH:
                    split_hi0(i - TPB - 1)

            def evacuate_hi(slot, q):
                act.activation(yT_hi[q][:, :, :], ps_y[:, :, :], ACT.Copy).then_inc(s_eh, 1)

            act.wait_ge(s_tab, 1)
            act.wait_ge(s_tp, 1)
            evacuate_hi(0, 0)
            act.wait_ge(s_oi, 16 * NT)

            def step(slot, q, turn):
                act.wait_ge(s_tp, slot + 2)
                act.wait_ge(s_mm, slot + 1)
                evacuate_hi(slot + 1, 1 - q)
                nxt = entry(act, NXT, slot, E - 1)
                with act.If(nxt > 0):
                    dst = act.snap((nxt & 1) * WSZ)
                    for c in range(NCH):
                        act.wait_ge(s_w[c], nxt * 16 + 16)
                        act.activation(w_hi[:, bass.ds(dst + c * CW, CW)],
                                       stage[:, CK * c:CK * (c + 1), :].rearrange("p k h -> p (k h)"),
                                       ACT.Copy).then_inc(s_hi, 1)
                act.nop()

            slots(act, step)

        @block.vector
        def _(dve):
            n_steps = [0]

            def link(ins):
                n_steps[0] += 1
                ins.then_inc(s_v, 1)
                dve.wait_ge(s_v, n_steps[0])

            dve.sem_inc(s_free, 2)
            dve.wait_ge(s_par, 16 * 4)
            dve.reciprocal(dv(INV1), par[:, 0:1])
            dve.reciprocal(dv(INV2), par[:, 2:3])
            dve.tensor_scalar(dv(D1), par[:, 1:2], -1.0, QMID, ALU.mult, ALU.add)
            dve.tensor_scalar(dv(D2), par[:, 3:4], -1.0, QMID, ALU.mult, ALU.add).then_inc(s_inv, 1)
            dve.wait_ge(s_inv, 1)
            dve.wait_ge(s_const, 1)

            def derive():
                dve.wait_ge(s_tanh, 1)
                link(dve.tensor_scalar(dv(C1), dv(TX), par[:, 0:1], par[:, 2:3], ALU.mult, ALU.mult))
                dve.tensor_scalar(dv(C2), dv(TF), 1.0 / TOPK, None, ALU.mult)
                dve.tensor_scalar(dv(C1D1), dv(C1), dv(D1), None, ALU.mult)
                link(dve.tensor_scalar(dv(C1D2), dv(C1), dv(D2), None, ALU.mult))
                dve.tensor_scalar(dv(C1KDD), dv(C1D1), dv(D2), float(D), ALU.mult, ALU.mult).then_inc(s_drv, 1)
                dve.wait_ge(s_drv, 1)

            def stats(which, i, n_ready):
                for h in range(HB):
                    last = dve.bn_stats(st[:, which, h, :], xt[:, i, h * 512:(h + 1) * 512])
                link(last)
                last = dve.bn_aggr(mv[:, which, i, :], st[:, which, :, :].rearrange("p a b -> p (a b)"))
                if n_ready:
                    last.then_inc(s_var[which], 1)
                    dve.wait_ge(s_var[which], n_ready)
                else:
                    link(last)

            def scales(which, i, n, count):
                v = lambda c: lnv[:, which, c, i:i + n]
                mean, var = mv[:, which, i:i + n, 0], mv[:, which, i:i + n, 1]
                dve.wait_ge(s_std[which], count)
                link(dve.reciprocal(v(RST), v(STD)))
                link(dve.scalar_tensor_tensor(v(T1), var, eps[:, :], v(RST), ALU.add, ALU.mult))
                link(dve.scalar_tensor_tensor(v(T2), v(T1), -0.5, v(RST), ALU.mult, ALU.mult))
                if which == 0:
                    link(dve.scalar_tensor_tensor(v(T1), v(T2), 1.5, v(RST), ALU.add, ALU.mult))
                    link(dve.tensor_scalar(v(AA), v(T1), dv(INV1), None, ALU.mult))
                    link(dve.scalar_tensor_tensor(v(T2), mean, -1.0, v(AA), ALU.mult, ALU.mult))
                    last = dve.tensor_scalar(v(BB), v(T2), par[:, 1:2], None, ALU.add)
                else:
                    link(dve.scalar_tensor_tensor(v(AA), v(T2), 1.5, v(RST), ALU.add, ALU.mult))
                    last = dve.scalar_tensor_tensor(v(BB), mean, -1.0, v(AA), ALU.mult, ALU.mult)
                last.then_inc(s_ab[which], 1)
                dve.wait_ge(s_ab[which], count)

            def quantise_x(i):
                link(dve.tensor_scalar(u8x[:, i % 2, :], xt[:, i, :], lnv[:, 0, AA, i:i + 1], lnv[:, 0, BB, i:i + 1],
                                       ALU.mult, ALU.add))
                if i >= 2:
                    dve.wait_ge(s_qt, i - 1)
                dve.tensor_scalar(q1[:, i % 2, :], u8x[:, i % 2, :], 1.0, -QMID, ALU.mult, ALU.add).then_inc(s_q1, 1)

            def x_new(i):
                dve.wait_ge(s_att, i + 2 + i // TPB)
                dve.wait_ge(s_xc, i + 1)
                dve.scalar_tensor_tensor(xt[:, i, :], ps[(i + 1 + i // TPB) % 2][:, :], dv(C1), xt[:, i, :],
                                         ALU.mult, ALU.add).then_inc(s_xn, 1)
                dve.wait_ge(s_xn, i + 1)

            def read_rowsums():
                dve.tensor_scalar(rsum[:, :], ps_s[:, RS_C:RS_C + NT], dv(C1D2), None, ALU.mult).then_inc(s_rs, 1)
                dve.wait_ge(s_rs, 1)
                dve.sem_inc(s_sread, 1)

            def select(b):
                r = slice(b * TPB, (b + 1) * TPB)
                g0 = GT_C + b * TPB * E
                dve.tensor_tensor(lg[:, :, :], ps_s[:, g0:g0 + TPB * E].rearrange("p (i e) -> p i e", e=E),
                                  bg[:, :].unsqueeze(1).to_broadcast([P, TPB, E]), ALU.add).then_inc(s_sread, 1)
                dve.wait_ge(s_sread, 2 * b + 2)
                other = lg[:, :, :].unsqueeze(2).to_broadcast([P, TPB, E, E])
                own = lg[:, :, :].unsqueeze(3).to_broadcast([P, TPB, E, E])
                first = tri[:, 0:E, :].unsqueeze(1).to_broadcast([P, TPB, E, E])
                link(dve.tensor_tensor(pw[:, 1], other, own, ALU.is_equal))
                dve.tensor_tensor(pw[:, 0], other, own, ALU.is_gt)
                link(dve.tensor_tensor(pw[:, 2], pw[:, 1], first, ALU.mult))
                link(dve.tensor_tensor(pw[:, 3], pw[:, 2], pw[:, 0], ALU.add))
                link(dve.tensor_reduce(rank[:, :, :], pw[:, 3], axis=AX.X, op=ALU.add))
                dve.tensor_scalar(sel[:, r, :], rank[:, :, :], float(TOPK), None, ALU.is_lt).then_inc(s_sel, 1)
                dve.wait_ge(s_sel, b + 1)
                link(dve.tensor_scalar(flip[:, :, :], sel[:, r, :], -2.0, 1.0, ALU.mult, ALU.add))
                dve.tensor_tensor(sgn[:, r, :], flip[:, :, :], tok1[:, r].unsqueeze(2).to_broadcast([P, TPB, E]), ALU.mult)
                link(dve.scalar_tensor_tensor(nback[:, :, :], rank[:, :, :], float(TOPK),
                                              back[:, r].unsqueeze(2).to_broadcast([P, TPB, E]), ALU.is_ge, ALU.mult))

            def positions(b):
                r = slice(b * TPB, (b + 1) * TPB)
                c0 = CU_C + b * TPB * E
                link(dve.tensor_tensor(pos[:, :, :], nback[:, :, :],
                                       ps_s[:, c0:c0 + TPB * E].rearrange("p (i e) -> p i e", e=E), ALU.add))
                if b == 0:
                    dve.sem_inc(s_sread, 1)
                link(dve.tensor_scalar(pH[:, r, :], pos[:, :, :], 1.0 / P, -0.498, ALU.mult, ALU.add))
                link(dve.scalar_tensor_tensor(pL[:, r, :], pH[:, r, :], -float(P), pos[:, :, :], ALU.mult, ALU.add))

            def make_onehots(b):
                for i in range(b * TPB, (b + 1) * TPB):
                    dve.tensor_tensor(onehot[i][:, :, :], pL[:, i, :].unsqueeze(1).to_broadcast([P, P, E]),
                                      iota_pe[:, :, :], ALU.is_equal).then_inc(s_oh, 1)

            def slot_matrix(b):
                r = slice(b * TPB * E, (b + 1) * TPB * E)
                rows = slice(b * TPB, (b + 1) * TPB)
                per_slot = lambda a: a[:, rows, :].rearrange("p i e -> p (i e)").unsqueeze(2).to_broadcast([P, TPB * E, SPE])
                link(dve.tensor_tensor(cmp[:, r, :], per_slot(pH),
                                       iota_f[:, 0:SPE].unsqueeze(1).to_broadcast([P, TPB * E, SPE]), ALU.is_equal))
                dve.tensor_tensor(R[:, r, :], cmp[:, r, :], per_slot(sgn), ALU.mult).then_inc(s_R, 1)

            def x_stats(i):
                dve.wait_ge(s_x[i], 16)
                stats(0, i, i // 2 + 1 if i % 2 else 0)

            x_stats(0)
            x_stats(1)
            x_stats(2)
            scales(0, 0, 2, 1)
            quantise_x(0)
            quantise_x(1)
            x_stats(3)
            derive()
            scales(0, 2, 2, 2)
            quantise_x(2)
            quantise_x(3)
            x_stats(4)
            x_stats(5)
            scales(0, 4, 2, 3)
            x_stats(6)
            x_stats(7)
            scales(0, 6, 2, 4)
            for i in range(NT):
                x_new(i)
                stats(1, i, i + 1)
                if i == TPB - 1:
                    dve.wait_ge(s_small, TPB)
                    read_rowsums()
                scales(1, i, 1, i + 1)
                if i == TPB + 1:
                    dve.wait_ge(s_small, TPB + 2)
                    select(0)
                if i == TPB + 2:
                    dve.wait_ge(s_cnt, 1)
                    positions(0)
            slot_matrix(0)
            dve.wait_ge(s_iota, 1)
            make_onehots(0)
            dve.wait_ge(s_small, NT + 2)
            select(1)
            dve.wait_ge(s_cnt, 2)
            positions(1)
            count, base_, rest = cnt[:, 0, :], cnt[:, 1, :], cnt[:, 2, :]
            link(dve.tensor_scalar(cnt8[:, :], ps_s[:, CU_C + NT * E:CU_C + (NT + 1) * E], 1.0 / P, 0.494, ALU.mult, ALU.add))
            slot_matrix(1)
            make_onehots(1)

            link(dve.tensor_scalar(count[:, 0:E], cnt8[:, :], 1.0, None, ALU.max))
            dve.tensor_scalar(rest[:, 0:E], count[:, 0:E], -1.0, float(SPE), ALU.mult, ALU.add)
            link(dve.tensor_tensor(tri9[:, :, :], tri[:, :, :], count[:, 0:E].unsqueeze(1).to_broadcast([P, E + 1, E]), ALU.mult))
            link(dve.tensor_reduce(base_[:, 0:E + 1], tri9[:, :, :], axis=AX.X, op=ALU.add))
            slot_no = iota_f[:, 0:NS].unsqueeze(2).to_broadcast([P, NS, E - 1])
            ends = base_[:, 1:E].unsqueeze(1).to_broadcast([P, NS, E - 1])
            starts = base_[:, 0:E - 1].unsqueeze(1).to_broadcast([P, NS, E - 1])
            per_expert = lambda a: a.unsqueeze(1).to_broadcast([P, NS, E - 1])
            link(dve.tensor_tensor(sc[:, 0], slot_no, ends, ALU.is_ge))
            dve.tensor_reduce(sv[:, 0, :], sc[:, 0], axis=AX.X, op=ALU.add)
            link(dve.tensor_tensor(sc[:, 1], sc[:, 0], per_expert(rest[:, 0:E - 1]), ALU.mult))
            link(dve.tensor_reduce(sv[:, 1, :], sc[:, 1], axis=AX.X, op=ALU.add))
            dve.tensor_tensor(tab[:, COL:COL + NS], sv[:, 1, :], iota_f[:, 0:NS], ALU.add).then_inc(s_col, 1)
            dve.wait_ge(s_idx_ps, 1)
            tok = tokens[:, 0, :]
            link(dve.tensor_copy(tok, ps_s[:, 0:E * SPE]))
            link(dve.scalar_tensor_tensor(tokens[:, 1, :], tok, -1.0, tok, ALU.mult, ALU.max))
            dve.tensor_scalar(idx[:, 0:E * SPE], tokens[:, 1, :], 1.0, -1.0, ALU.max, ALU.add).then_inc(s_idx, 1)
            link(dve.tensor_tensor(sc[:, 0], slot_no, starts, ALU.is_equal))
            link(dve.tensor_tensor(sc[:, 1], sc[:, 0], per_expert(iota_f[:, 1:E]), ALU.mult))
            link(dve.tensor_reduce(sv[:, 4, :], sc[:, 1], axis=AX.X, op=ALU.add))
            dve.tensor_copy(tab[:, NXT:NXT + NS], sv[:, 4, :])
            dve.tensor_scalar(weight[:, :], tokens[:, 0, :], 0.0, dv(C2), ALU.is_lt, ALU.mult)
            link(dve.tensor_scalar(svi[:, :], sv[:, 0, :], 0.5, -0.25, ALU.mult, ALU.add))
            link(dve.tensor_copy(sv[:, 2, :], svi[:, :]))
            link(dve.scalar_tensor_tensor(sv[:, 3, :], sv[:, 2, :], -2.0, sv[:, 0, :], ALU.mult, ALU.add))
            dve.tensor_copy(tab[:, EXPERT:EXPERT + NS], sv[:, 0, :])
            dve.tensor_scalar(tab[:, WOFF:WOFF + NS], sv[:, 3, :], float(WSZ), None, ALU.mult)
            dve.tensor_copy(tab[:, BAS:BAS + E + 1], base_[:, 0:E + 1]).then_inc(s_tab, 1)
            dve.wait_ge(s_idx, 1)
            dve.wait_ge(s_tab, 1)

            def evacuate_lo(q):
                dve.tensor_tensor(yT_lo[q][:, :, :], ps_y[:, :, :], yT_hi[q][:, :, :].bitcast(f32),
                                  ALU.subtract).then_inc(s_el, 1)

            def split_lo(c, chunk_no, dst):
                dve.wait_ge(s_hi, chunk_no)
                dve.tensor_tensor(w_lo[:, dst], stage[:, CK * c:CK * (c + 1), :].rearrange("p k h -> p (k h)"),
                                  w_hi[:, dst].bitcast(f32), ALU.subtract).then_inc(s_lo, 1)

            dve.wait_ge(s_eh, 1)
            evacuate_lo(0)
            dve.wait_ge(s_lo, NLO)
            dve.wait_ge(s_oi, 16 * NT)

            def step(slot, q, turn):
                dve.wait_ge(s_eh, slot + 2)
                evacuate_lo(1 - q)
                nxt = entry(dve, NXT, slot, E - 1)
                with dve.If(nxt > 0):
                    dst = dve.snap((nxt & 1) * WSZ)
                    for c in range(NLO):
                        split_lo(c, nxt * NCH + c + 1, bass.ds(dst + c * CW, CW))
                woff = entry(dve, WOFF, slot, WSZ)
                expert = entry(dve, EXPERT, slot, E - 1)
                for b in range(2):
                    with dve.If(woff == b * WSZ):
                        dve.wait_ge(s_bias[b], ((expert + 2) >> 1) * 16)
                        settle(dve)
                col = entry(dve, COL, slot, E * SPE - 1)
                dve.wait_ge(s_mm, slot + 2)
                dve.wait_ge(s_resf, slot + 1)
                dve.tensor_tensor(res[q][:, :], ps[q][:, :], bias[:, bass.ds(woff >> 3, D)], ALU.add).then_inc(s_free, 1)
                dve.wait_ge(s_free, slot + 3)
                dve.tensor_scalar(res[q][:, :], res[q][:, :], 0.0, weight[:, bass.ds(col, 1)],
                                  ALU.max, ALU.mult).then_inc(s_post, 1)

            slots(dve, step)

        @block.tensor
        def _(pe):
            pe.wait_ge(s_const, 1)

            def transpose_q1(i):
                pe.wait_ge(s_q1, i + 1)
                if i >= 1:
                    pe.wait_ge(s_qe, i)
                for k in range(KT):
                    last = pe.transpose(ps_q[:, k, :], q1[:, i % 2, k * P:(k + 1) * P], ident_b[:, :])
                last.then_inc(s_qt, 1)

            def column_sums(b):
                u = b * (TPB + 1)
                if u >= 2:
                    pe.wait_ge(s_xn, u - 2)
                for k in range(KT):
                    pe.wait_ge(s_q2, b * KT + k + 1)
                    for h in range(HB):
                        last = pe.matmul(ps[u % 2][:, h * 512:(h + 1) * 512], ones_b[:, :],
                                         q2[:, b * KT + k, h * 512:(h + 1) * 512], start=(k == 0), stop=(k == KT - 1))
                last.then_inc(s_att, 1)

            def attention(i):
                b = i // TPB
                u = i + 1 + b
                if u == 2 or u == TPB + 3:
                    pe.wait_ge(s_corr, b + 1)
                if i >= 2 and u != TPB + 3:
                    pe.wait_ge(s_xn, i - 1 if i != TPB else TPB)
                pe.wait_ge(s_qe, i + 1)
                for k in range(KT):
                    for h in range(HB):
                        last = pe.matmul(ps[u % 2][:, h * 512:(h + 1) * 512], q1T[:, i, k, :],
                                         q2[:, b * KT + k, h * 512:(h + 1) * 512], start=(k == 0), stop=(k == KT - 1))
                last.then_inc(s_att, 1)

            def transpose_y(i):
                pe.wait_ge(s_y, i + 1)
                if i >= 1:
                    pe.wait_ge(s_ye, i)
                for k in range(KT):
                    last = pe.transpose(ps_y[:, k, :], y[i % 2][:, k * P:(k + 1) * P], ident_f[:, :])
                last.then_inc(s_yt, 1)

            def rowsum(i):
                pe.wait_ge(s_qe, i + 1)
                for k in range(KT):
                    last = pe.matmul(ps_s[:, RS_C + i:RS_C + i + 1], q1T[:, i, k, :], ones_b[:, 0:1],
                                     start=(k == 0), stop=(k == KT - 1))
                return last

            def small(i):
                for group, reads in ((TPB, 1), (TPB + 2, 2), (TPB + 3, 3)):
                    if i == group:
                        pe.wait_ge(s_sread, reads)
                if i < TPB:
                    last = rowsum(i)
                if i == TPB - 1:
                    for j in range(TPB, NT):
                        last = rowsum(j)
                if 2 <= i:
                    pe.wait_ge(s_ye, i - 1)
                    g = GT_C + (i - 2) * E
                    for k in range(KT):
                        last = pe.matmul(ps_s[:, g:g + E], yT[i % 2][:, k, :], wg[:, k, :],
                                         start=(k == 0), stop=(k == KT - 1))
                last.then_inc(s_small, 1)

            def counts(b):
                first, end = b * TPB, TPB if b == 0 else NT + 1
                pe.wait_ge(s_sel, b + 1)
                cols = lambda a: ps_s[:, CU_C + a * E:CU_C + end * E].rearrange("p (i e) -> p i e", e=E)
                pe.matmul(cols(first), before[:, :], sel[:, first:end, :], start=True, stop=False)
                for j in range(min(end - 1, NT)):
                    a = max(first, j + 1)
                    last = pe.matmul(cols(a), ones_b[:, :], sel[:, j:j + 1, :].to_broadcast([P, end - a, E]),
                                     start=False, stop=(j == min(end - 1, NT) - 1))
                last.then_inc(s_cnt, 1)

            for i in range(TPB):
                transpose_q1(i)
            column_sums(0)
            for i in range(NT + 2):
                if i == TPB:
                    column_sums(1)
                if i < NT:
                    attention(i)
                if i == 2:
                    pe.wait_ge(s_wg, 16)
                small(i)
                if i in (1, 2):
                    transpose_q1(TPB + 2 * i - 2)
                    transpose_q1(TPB + 2 * i - 1)
                if 1 <= i <= NT:
                    transpose_y(i - 1)
                if i == TPB + 2:
                    counts(0)
            counts(1)
            pe.wait_ge(s_R, 2)
            pe.matmul(ps_s[:, 0:E * SPE].rearrange("p (a b) -> p a b", b=E), ones_b[:, :],
                      sel[:, NT:NT + 1, :].to_broadcast([P, SPE, E]), start=True, stop=False)
            for i in range(NT):
                pe.wait_ge(s_oh, i + 1)
                for e in range(E):
                    last = pe.matmul(ps_s[:, e * SPE:(e + 1) * SPE], onehot[i][:, :, e], R[:, i * E + e, :],
                                     start=False, stop=(i == NT - 1 and e == E - 1))
            last.then_inc(s_idx_ps, 1)

            def transpose_slot(q):
                for k in range(KT):
                    last = pe.transpose(ps_y[:, k, :], y_rows[q][:, k * P:(k + 1) * P], ident_f[:, :])
                last.then_inc(s_tp, 1)

            pe.wait_ge(s_tab, 1)
            pe.wait_ge(s_idx_ps, 1)
            pe.sem_inc(s_mm, 1)
            pe.wait_ge(s_g[0], 16)
            transpose_slot(0)

            def step(slot, q, turn):
                pe.wait_ge(s_g[1 - q], turn * 16 + (16 if q == 0 else 32))
                pe.wait_ge(s_el, slot + 1)
                transpose_slot(1 - q)
                expert = entry(pe, EXPERT, slot, E - 1)
                woff = entry(pe, WOFF, slot, WSZ)
                pe.wait_ge(s_free, slot + 1)
                for k in range(KT):
                    if k % CK == 0 and k < NLO * CK:
                        pe.wait_ge(s_lo, expert * NLO + (k // CK + 1))
                    elif k % CK == 0:
                        pe.wait_ge(s_lop, expert + 1)
                    for lhs, w in ((yT_hi, w_hi), (yT_hi, w_lo), (yT_lo, w_hi)):
                        for h in range(HB):
                            last = pe.matmul(ps[q][:, h * 512:(h + 1) * 512], lhs[q][:, k, :],
                                             w[:, bass.ds(woff + k * D + h * 512, 512)],
                                             start=(k == 0 and lhs is yT_hi and w is w_hi),
                                             stop=(k == KT - 1 and lhs is yT_lo))
                last.then_inc(s_mm, 1)

            slots(pe, step)


_INS = ["x", "ctx_4096", "g_xattn", "g_ffn", "L0_xattn_x1_scale", "L0_xattn_x1_zp", "L0_xattn_x2_scale",
        "L0_xattn_x2_zp", "L0_ffn_W_gate", "L0_ffn_b_gate", "L0_ffn_W_e", "L0_ffn_b_e"]
_OUTS = [((2, 512, 1024), "float32")]


def kernel(**inputs):
    import numpy as _np
    import concourse.bacc as _bacc
    from concourse import mybir as _mybir
    from concourse.bass_utils import run_bass_kernel_spmd as _run

    nc = _bacc.Bacc("TRN2", target_bir_lowering=False, num_devices=1)
    arrays, args = {}, []
    for name in _INS:
        a = _np.ascontiguousarray(inputs[name])
        arrays[f"in_{name}_dram"] = a
        args.append(nc.dram_tensor(f"in_{name}_dram", a.shape, _mybir.dt.from_np(a.dtype), kind="ExternalInput").ap())
    for i, (shape, dtype) in enumerate(_OUTS):
        dt = _mybir.dt.from_np(_np.dtype(dtype))
        args.append(nc.dram_tensor(f"out_{i}_dram", shape, dt, kind="ExternalOutput").ap())
    flamingo_gated_moe(nc, *args)
    r = _run(nc, [arrays], core_ids=[0])
    got = tuple(r.results[0][f"out_{i}_dram"] for i in range(len(_OUTS)))
    return got[0]
```
